# Optimizing a Trainium2 kernel written in Bass

```python
import numpy as np
import jax
import jax.numpy as jnp

def _softmax(x, axis=-1):
    return jax.nn.softmax(x, axis=axis)

def _gelu(x):
    return jax.nn.gelu(x, approximate=True)

def _silu(x):
    return jax.nn.silu(x)

def _sigmoid(x):
    return jax.nn.sigmoid(x)

def _layernorm(x, axis=-1, eps=1e-05):
    m = jnp.mean(x, axis=axis, keepdims=True)
    v = jnp.var(x, axis=axis, keepdims=True)
    return (x - m) / jnp.sqrt(v + eps)

def _scatter_add(tgt, idx, src, axis=0):
    return tgt.at[idx].add(src)

def _segment_sum(src, seg, n):
    return jax.ops.segment_sum(src, seg, n)
kernel_name = 'mk_adj_resnorm_d4_adj_r2_706217'

def setup_inputs(seed: int=0):
    np.random.seed(seed)
    _w = jnp.asarray

    def _rec_inputs():
        import jax
        import jax.numpy as jnp
        _gk = jax.random.key(seed)
        x = -0.0005207 + 1.001 * jax.random.normal(jax.random.fold_in(_gk, 1), (32, 256, 128), jnp.float32)
        _w = (1.0 + jnp.arange(256, dtype=jnp.float32)) ** (-0.5)
        _w = _w / _w.mean()
        _pij = jnp.clip(0.0078125 * _w[:, None] * _w[None, :], 0.0, 1.0)
        _a = jax.random.uniform(jax.random.fold_in(_gk, 2), (256, 256)) < _pij
        _a = jnp.logical_or(_a, jnp.swapaxes(_a, -1, -2))
        _a = jnp.logical_or(_a, jnp.eye(256, dtype=bool))
        _af = _a.astype(jnp.float32)
        _af = _af * jax.random.uniform(jax.random.fold_in(_gk, 3), (256, 256), jnp.float32, 0.05, 32)
        adj = _af
        return (x, adj)
    x, adj = _rec_inputs()

    def _L0_gnn_setup():
        import jax, jax.numpy as jnp
        import numpy as np
        EPS_LN = 1e-05

        def _layernorm(x, g, b):
            mu = x.mean(-1, keepdims=True)
            var = ((x - mu) ** 2).mean(-1, keepdims=True)
            return (x - mu) / jnp.sqrt(var + EPS_LN) * g + b
        key = jax.random.key(seed)
        B, N, D, H = (4, 1024, 128, 4)
        hid = int(D * 2.0)
        ks = jax.random.split(key, 12)
        x = jax.random.normal(ks[0], (B, N, D), jnp.float32)
        Au = jax.random.uniform(ks[1], (N, N)) < 0.004
        A = jnp.logical_or(Au, Au.T)
        A = A.at[jnp.arange(N), jnp.arange(N)].set(False)
        Af = A.astype(jnp.float32)
        deg = Af.sum(axis=1)
        L = jnp.diag(deg) - Af
        adjacency = Af + jnp.eye(N, dtype=jnp.float32)
        s = lambda k, sh, f: jax.random.normal(k, sh, jnp.float32) * f
        sc = 1.0 / np.sqrt(D)
        Wc = s(ks[2], (D, D), sc)
        bc = jnp.zeros((D,), jnp.float32)
        Wq = s(ks[3], (D, D), sc)
        Wk = s(ks[4], (D, D), sc)
        Wv = s(ks[5], (D, D), sc)
        Wo = s(ks[6], (D, D), sc)
        bo = jnp.zeros((D,), jnp.float32)
        W1 = s(ks[7], (D, hid), sc)
        b1 = jnp.zeros((hid,), jnp.float32)
        W2 = s(ks[8], (hid, D), 1.0 / np.sqrt(hid))
        b2 = jnp.zeros((D,), jnp.float32)
        g1 = jnp.ones((D,), jnp.float32)
        be1 = jnp.zeros((D,), jnp.float32)
        g2 = jnp.ones((D,), jnp.float32)
        be2 = jnp.zeros((D,), jnp.float32)
        g3 = jnp.ones((D,), jnp.float32)
        be3 = jnp.zeros((D,), jnp.float32)
        return dict(x=x, L=L, adjacency=adjacency, Wc=Wc, bc=bc, g1=g1, be1=be1, Wq=Wq, Wk=Wk, Wv=Wv, Wo=Wo, bo=bo, g2=g2, be2=be2, W1=W1, b1=b1, W2=W2, b2=b2, g3=g3, be3=be3)
    _L0_gnn_all = _L0_gnn_setup()
    _L0_gnn_in = {k: v for k, v in _L0_gnn_all.items() if k in ('Wc', 'bc', 'g1', 'be1', 'Wq', 'Wk', 'Wv', 'Wo', 'bo', 'g2', 'be2', 'W1', 'b1', 'W2', 'b2', 'g3', 'be3')}
    del _L0_gnn_all

    def _L1_gnn_setup():
        import jax, jax.numpy as jnp
        import numpy as np
        EPS = 1e-05

        def _batchnorm(x, gamma, beta):
            mu = jnp.mean(x, axis=0)
            var = jnp.var(x, axis=0)
            return (x - mu) * jax.lax.rsqrt(var + EPS) * gamma + beta
        key = jax.random.key(seed)
        ks = jax.random.split(key, 4)
        b, n, d, h, o = (32, 1024, 128, 256, 128)
        features = jax.random.normal(ks[0], (b, n, d), dtype=jnp.float32)
        A = jax.random.uniform(ks[1], (n, n), dtype=jnp.float32)
        lim1 = float(np.sqrt(6.0 / (d + h)))
        W1 = jax.random.uniform(ks[2], (h, d), minval=-lim1, maxval=lim1, dtype=jnp.float32)
        b1 = jnp.zeros((h,), jnp.float32)
        lim2 = float(np.sqrt(6.0 / (h + o)))
        W2 = jax.random.uniform(ks[3], (o, h), minval=-lim2, maxval=lim2, dtype=jnp.float32)
        b2 = jnp.zeros((o,), jnp.float32)
        g1 = jnp.ones((h,), jnp.float32)
        be1 = jnp.zeros((h,), jnp.float32)
        g2 = jnp.ones((o,), jnp.float32)
        be2 = jnp.zeros((o,), jnp.float32)
        return {'features': features, 'A': A, 'W1': W1, 'b1': b1, 'g1': g1, 'be1': be1, 'W2': W2, 'b2': b2, 'g2': g2, 'be2': be2}
    _L1_gnn_all = _L1_gnn_setup()
    _L1_gnn_in = {k: v for k, v in _L1_gnn_all.items() if k in ('W1', 'b1', 'g1', 'be1', 'W2', 'b2', 'g2', 'be2')}
    del _L1_gnn_all

    def _L2_gnn_setup():
        import jax, jax.numpy as jnp
        import numpy as np
        B, N, D, H = (4, 2048, 128, 128)
        key = jax.random.key(seed)
        ks = jax.random.split(key, 10)
        base_features = jax.random.normal(ks[0], (B, N, D), dtype=jnp.float32)
        pc = (jax.random.uniform(ks[1], (N, N)) < 8.0 / N).astype(jnp.float32)
        pc = pc * (1.0 - jnp.eye(N, dtype=jnp.float32))
        neighbor_mask = jnp.clip(pc + pc.T + jnp.eye(N, dtype=jnp.float32), 0.0, 1.0)
        s = 1.0 / np.sqrt(D)
        Wq = jax.random.normal(ks[2], (D, H), dtype=jnp.float32) * s
        Wk = jax.random.normal(ks[3], (D, H), dtype=jnp.float32) * s
        Wv = jax.random.normal(ks[4], (D, H), dtype=jnp.float32) * s
        Wo = jax.random.normal(ks[5], (H, D), dtype=jnp.float32) * (1.0 / np.sqrt(H))
        bq = jnp.zeros((H,), jnp.float32)
        bk = jnp.zeros((H,), jnp.float32)
        bv = jnp.zeros((H,), jnp.float32)
        bo = jnp.zeros((D,), jnp.float32)
        alpha = jnp.asarray(2.0, jnp.float32)
        gamma = jnp.asarray(0.3, jnp.float32)
        return dict(base_features=base_features, neighbor_mask=neighbor_mask, parent_child_mask=pc, Wq=Wq, bq=bq, Wk=Wk, bk=bk, Wv=Wv, bv=bv, Wo=Wo, bo=bo, alpha=alpha, gamma=gamma)
    _L2_gnn_all = _L2_gnn_setup()
    _L2_gnn_in = {k: v for k, v in _L2_gnn_all.items() if k in ('Wq', 'bq', 'Wk', 'bk', 'Wv', 'bv', 'Wo', 'bo', 'alpha', 'gamma')}
    del _L2_gnn_all

    def _L3_gnn_setup():
        import jax, jax.numpy as jnp
        import numpy as np
        B, T, D, H = (64, 1024, 128, 128)
        MAX_SKIP = 4

        def _lstm_last(Wih, Whh, bih, bhh, xs):
            N, _, Hd = xs.shape
            bias = bih + bhh

            def step(carry, x_t):
                h, c = carry
                g = x_t @ Wih.T + h @ Whh.T + bias
                i, f, gg, o = jnp.split(g, 4, axis=-1)
                c = jax.nn.sigmoid(f) * c + jax.nn.sigmoid(i) * jnp.tanh(gg)
                h = jax.nn.sigmoid(o) * jnp.tanh(c)
                return ((h, c), None)
            init = (jnp.zeros((N, Hd), xs.dtype), jnp.zeros((N, Hd), xs.dtype))
            (h_last, _), _ = jax.lax.scan(step, init, jnp.swapaxes(xs, 0, 1))
            return h_last
        key = jax.random.key(seed)
        ks = jax.random.split(key, 8)
        s = 0.05
        x = jax.random.normal(ks[0], (B, T, D), jnp.float32)
        adj = jax.random.uniform(ks[1], (T, T), jnp.float32) / T
        Wg0 = jax.random.normal(ks[2], (D, H), jnp.float32) * s
        bg0 = jnp.zeros((H,), jnp.float32)
        Wg1 = jax.random.normal(ks[3], (H, H), jnp.float32) * s
        bg1 = jnp.zeros((H,), jnp.float32)
        Wih = jax.random.normal(ks[4], (MAX_SKIP, 4 * H, H), jnp.float32) * s
        Whh = jax.random.normal(ks[5], (MAX_SKIP, 4 * H, H), jnp.float32) * s
        bih = jax.random.normal(ks[6], (MAX_SKIP, 4 * H), jnp.float32) * s
        bhh = jax.random.normal(ks[7], (MAX_SKIP, 4 * H), jnp.float32) * s
        return dict(x=x, adj=adj, Wg0=Wg0, bg0=bg0, Wg1=Wg1, bg1=bg1, Wih=Wih, Whh=Whh, bih=bih, bhh=bhh)
    _L3_gnn_all = _L3_gnn_setup()
    _L3_gnn_in = {k: v for k, v in _L3_gnn_all.items() if k in ('Wg0', 'bg0', 'Wg1', 'bg1', 'Wih', 'Whh', 'bih', 'bhh')}
    del _L3_gnn_all
    return {'x': x, 'adj': adj, 'L0_gnn_Wc': _L0_gnn_in['Wc'], 'L0_gnn_bc': _L0_gnn_in['bc'], 'L0_gnn_g1': _L0_gnn_in['g1'], 'L0_gnn_be1': _L0_gnn_in['be1'], 'L0_gnn_Wq': _L0_gnn_in['Wq'], 'L0_gnn_Wk': _L0_gnn_in['Wk'], 'L0_gnn_Wv': _L0_gnn_in['Wv'], 'L0_gnn_Wo': _L0_gnn_in['Wo'], 'L0_gnn_bo': _L0_gnn_in['bo'], 'L0_gnn_g2': _L0_gnn_in['g2'], 'L0_gnn_be2': _L0_gnn_in['be2'], 'L0_gnn_W1': _L0_gnn_in['W1'], 'L0_gnn_b1': _L0_gnn_in['b1'], 'L0_gnn_W2': _L0_gnn_in['W2'], 'L0_gnn_b2': _L0_gnn_in['b2'], 'L0_gnn_g3': _L0_gnn_in['g3'], 'L0_gnn_be3': _L0_gnn_in['be3'], 'L1_gnn_W1': _L1_gnn_in['W1'], 'L1_gnn_b1': _L1_gnn_in['b1'], 'L1_gnn_g1': _L1_gnn_in['g1'], 'L1_gnn_be1': _L1_gnn_in['be1'], 'L1_gnn_W2': _L1_gnn_in['W2'], 'L1_gnn_b2': _L1_gnn_in['b2'], 'L1_gnn_g2': _L1_gnn_in['g2'], 'L1_gnn_be2': _L1_gnn_in['be2'], 'L2_gnn_Wq': _L2_gnn_in['Wq'], 'L2_gnn_bq': _L2_gnn_in['bq'], 'L2_gnn_Wk': _L2_gnn_in['Wk'], 'L2_gnn_bk': _L2_gnn_in['bk'], 'L2_gnn_Wv': _L2_gnn_in['Wv'], 'L2_gnn_bv': _L2_gnn_in['bv'], 'L2_gnn_Wo': _L2_gnn_in['Wo'], 'L2_gnn_bo': _L2_gnn_in['bo'], 'L2_gnn_alpha': _L2_gnn_in['alpha'], 'L2_gnn_gamma': _L2_gnn_in['gamma'], 'L3_gnn_Wg0': _L3_gnn_in['Wg0'], 'L3_gnn_bg0': _L3_gnn_in['bg0'], 'L3_gnn_Wg1': _L3_gnn_in['Wg1'], 'L3_gnn_bg1': _L3_gnn_in['bg1'], 'L3_gnn_Wih': _L3_gnn_in['Wih'], 'L3_gnn_Whh': _L3_gnn_in['Whh'], 'L3_gnn_bih': _L3_gnn_in['bih'], 'L3_gnn_bhh': _L3_gnn_in['bhh']}

def reference(x, adj, L0_gnn_Wc, L0_gnn_bc, L0_gnn_g1, L0_gnn_be1, L0_gnn_Wq, L0_gnn_Wk, L0_gnn_Wv, L0_gnn_Wo, L0_gnn_bo, L0_gnn_g2, L0_gnn_be2, L0_gnn_W1, L0_gnn_b1, L0_gnn_W2, L0_gnn_b2, L0_gnn_g3, L0_gnn_be3, L1_gnn_W1, L1_gnn_b1, L1_gnn_g1, L1_gnn_be1, L1_gnn_W2, L1_gnn_b2, L1_gnn_g2, L1_gnn_be2, L2_gnn_Wq, L2_gnn_bq, L2_gnn_Wk, L2_gnn_bk, L2_gnn_Wv, L2_gnn_bv, L2_gnn_Wo, L2_gnn_bo, L2_gnn_alpha, L2_gnn_gamma, L3_gnn_Wg0, L3_gnn_bg0, L3_gnn_Wg1, L3_gnn_bg1, L3_gnn_Wih, L3_gnn_Whh, L3_gnn_bih, L3_gnn_bhh):
    import jax
    import jax.numpy as jnp

    def _L0_gnn_ref(x, L, adjacency, Wc, bc, g1, be1, Wq, Wk, Wv, Wo, bo, g2, be2, W1, b1, W2, b2, g3, be3):
        import jax, jax.numpy as jnp
        import numpy as np
        EPS_LN = 1e-05

        def _layernorm(x, g, b):
            mu = x.mean(-1, keepdims=True)
            var = ((x - mu) ** 2).mean(-1, keepdims=True)
            return (x - mu) / jnp.sqrt(var + EPS_LN) * g + b
        B, N, D = x.shape
        H = 4
        hd = D // H
        eig = jnp.linalg.eigvalsh(L)
        lam_max = eig[-1] + 1e-08
        L_norm = 2.0 * L / lam_max - jnp.eye(N, dtype=L.dtype)
        xp = jnp.einsum('mn,bnf->bmf', L_norm, x)
        h = xp @ Wc + bc
        h = _layernorm(h, g1, be1)
        h = jax.nn.relu(h)
        x1 = h + x
        q = (x1 @ Wq).reshape(B, N, H, hd).transpose(0, 2, 1, 3)
        k = (x1 @ Wk).reshape(B, N, H, hd).transpose(0, 2, 1, 3)
        v = (x1 @ Wv).reshape(B, N, H, hd).transpose(0, 2, 1, 3)
        scores = jnp.einsum('bhnd,bhmd->bhnm', q, k) / np.sqrt(hd).astype(np.float32)
        scores = jnp.where(adjacency[None, None] > 0, scores, jnp.float32(-1000000000.0))
        attn = jax.nn.softmax(scores, axis=-1)
        o = jnp.einsum('bhnm,bhmd->bhnd', attn, v)
        o = o.transpose(0, 2, 1, 3).reshape(B, N, D)
        o = o @ Wo + bo
        x2 = _layernorm(x1 + o, g2, be2)
        m = jax.nn.gelu(x2 @ W1 + b1, approximate=False) @ W2 + b2
        return _layernorm(x2 + m, g3, be3)

    def _L1_gnn_ref(features, A, W1, b1, g1, be1, W2, b2, g2, be2):
        import jax, jax.numpy as jnp
        import numpy as np
        EPS = 1e-05

        def _batchnorm(x, gamma, beta):
            mu = jnp.mean(x, axis=0)
            var = jnp.var(x, axis=0)
            return (x - mu) * jax.lax.rsqrt(var + EPS) * gamma + beta
        b, n, d = features.shape
        A_norm = A + jnp.eye(n, dtype=A.dtype)
        deg = jnp.sum(A_norm, axis=0) + jnp.sum(A_norm, axis=1) - jnp.diagonal(A_norm)
        dinv = jax.lax.rsqrt(deg)
        A_hat = A_norm * dinv[:, None] * dinv[None, :]
        agg = jnp.einsum('nm,bmd->bnd', A_hat, features)
        x = agg.reshape(-1, d)
        h = jax.nn.relu(_batchnorm(x @ W1.T + b1, g1, be1))
        out = h @ W2.T + b2
        out = _batchnorm(out, g2, be2)
        return out.reshape(b, n, -1)

    def _L2_gnn_ref(base_features, neighbor_mask, parent_child_mask, Wq, bq, Wk, bk, Wv, bv, Wo, bo, alpha, gamma):
        import jax, jax.numpy as jnp
        import numpy as np
        B, N, D, H = (4, 2048, 128, 128)
        x = base_features
        Q = x @ Wq + bq
        K = x @ Wk + bk
        V = x @ Wv + bv
        scale = 1.0 / jnp.sqrt(jnp.asarray(K.shape[-1], x.dtype))
        scores = jnp.einsum('bnh,bmh->bnm', Q, K) * scale
        scores = scores + parent_child_mask[None] * alpha
        scores = jnp.where(neighbor_mask[None] == 0, jnp.asarray(-1000000000.0, x.dtype), scores)
        attn = jax.nn.softmax(scores, axis=-1)
        attn_out = jnp.einsum('bnm,bmh->bnh', attn, V)
        refined = attn_out @ Wo + bo + x
        child_sum = jnp.einsum('nm,bmd->bnd', parent_child_mask, refined)
        is_parent = (parent_child_mask.sum(axis=1) > 0).astype(x.dtype)
        delta = gamma * (child_sum - refined)
        return refined + delta * is_parent[None, :, None]

    def _L3_gnn_ref(x, adj, Wg0, bg0, Wg1, bg1, Wih, Whh, bih, bhh):
        import jax, jax.numpy as jnp
        import numpy as np
        B, T, D, H = (64, 1024, 128, 128)
        MAX_SKIP = 4

        def _lstm_last(Wih, Whh, bih, bhh, xs):
            N, _, Hd = xs.shape
            bias = bih + bhh

            def step(carry, x_t):
                h, c = carry
                g = x_t @ Wih.T + h @ Whh.T + bias
                i, f, gg, o = jnp.split(g, 4, axis=-1)
                c = jax.nn.sigmoid(f) * c + jax.nn.sigmoid(i) * jnp.tanh(gg)
                h = jax.nn.sigmoid(o) * jnp.tanh(c)
                return ((h, c), None)
            init = (jnp.zeros((N, Hd), xs.dtype), jnp.zeros((N, Hd), xs.dtype))
            (h_last, _), _ = jax.lax.scan(step, init, jnp.swapaxes(xs, 0, 1))
            return h_last
        h = jax.nn.relu(jnp.einsum('ts,bsh->bth', adj, x @ Wg0 + bg0))
        h = jax.nn.relu(jnp.einsum('ts,bsh->bth', adj, h @ Wg1 + bg1))
        Bv, Tv, Hd = h.shape
        for p in range(1, MAX_SKIP + 1):
            nw = Tv // p
            wins = h[:, :nw * p, :].reshape(Bv * nw, p, Hd)
            last = _lstm_last(Wih[p - 1], Whh[p - 1], bih[p - 1], bhh[p - 1], wins)
            idx = jnp.arange(nw) * p + (p - 1)
            h = h.at[:, idx, :].set(last.reshape(Bv, nw, Hd))
        return h
    x = _layernorm(x + _L0_gnn_ref(x, adj, adj, L0_gnn_Wc, L0_gnn_bc, L0_gnn_g1, L0_gnn_be1, L0_gnn_Wq, L0_gnn_Wk, L0_gnn_Wv, L0_gnn_Wo, L0_gnn_bo, L0_gnn_g2, L0_gnn_be2, L0_gnn_W1, L0_gnn_b1, L0_gnn_W2, L0_gnn_b2, L0_gnn_g3, L0_gnn_be3), axis=-1)
    x = _layernorm(x + _L1_gnn_ref(x, adj, L1_gnn_W1, L1_gnn_b1, L1_gnn_g1, L1_gnn_be1, L1_gnn_W2, L1_gnn_b2, L1_gnn_g2, L1_gnn_be2), axis=-1)
    x = _layernorm(x + _L2_gnn_ref(x, adj, adj, L2_gnn_Wq, L2_gnn_bq, L2_gnn_Wk, L2_gnn_bk, L2_gnn_Wv, L2_gnn_bv, L2_gnn_Wo, L2_gnn_bo, L2_gnn_alpha, L2_gnn_gamma), axis=-1)
    x = _layernorm(x + _L3_gnn_ref(x, adj, L3_gnn_Wg0, L3_gnn_bg0, L3_gnn_Wg1, L3_gnn_bg1, L3_gnn_Wih, L3_gnn_Whh, L3_gnn_bih, L3_gnn_bhh), axis=-1)
    return x

_drawn_inputs = setup_inputs


def setup_inputs(seed=0):
    import zlib

    import numpy as np

    out = dict(_drawn_inputs(seed))
    spreads = {'L0_gnn_bc': (0.0, 0.1),
     'L0_gnn_g1': (1.0, 0.2),
     'L0_gnn_be1': (0.0, 0.1),
     'L0_gnn_bo': (0.0, 0.1),
     'L0_gnn_g2': (1.0, 0.2),
     'L0_gnn_be2': (0.0, 0.1),
     'L0_gnn_b1': (0.0, 0.1),
     'L0_gnn_b2': (0.0, 0.1),
     'L0_gnn_g3': (1.0, 0.2),
     'L0_gnn_be3': (0.0, 0.1),
     'L1_gnn_b1': (0.0, 0.8),
     'L1_gnn_g1': (1.0, 0.2),
     'L1_gnn_be1': (0.0, 0.1),
     'L1_gnn_b2': (0.0, 0.8),
     'L1_gnn_g2': (1.0, 0.2),
     'L1_gnn_be2': (0.0, 0.1),
     'L2_gnn_bq': (0.0, 0.482),
     'L2_gnn_bk': (0.0, 0.8),
     'L2_gnn_bv': (0.0, 0.1),
     'L2_gnn_bo': (0.0, 0.1),
     'L3_gnn_bg0': (0.0, 0.1),
     'L3_gnn_bg1': (0.0, 0.337)}
    factors = {'L3_gnn_Whh': 7.5, 'L3_gnn_bih': 3.138, 'L3_gnn_bhh': 3.216}
    for name, (base, spread) in spreads.items():
        noise = np.random.default_rng([zlib.crc32(name.encode()), seed]).standard_normal(out[name].shape)
        drawn = base * np.exp(spread * noise) if base else spread * noise
        out[name] = jnp.asarray(drawn.astype(out[name].dtype))
    for name, factor in factors.items():
        out[name] = (out[name] * factor).astype(out[name].dtype)
    return out
```

```python
from contextlib import ExitStack

import concourse.bass as bass
from concourse import mybir

P = 128
B = 32
N = 256
J = N // P
D = 128
HEADS = 4
HD = D // HEADS
HC = 2
COPIES = 4
SQUARINGS = 15
GROUP = 3
CH = 512
NCH = B * N // CH
GB = 4
GC = GB * N
NG = B // GB
SKIP = 4
GATES = 4
EPS = 1e-5
MASKED = -1e9

ALU = mybir.AluOpType
ACT = mybir.ActivationFunctionType
F32 = mybir.dt.float32
F32R = mybir.dt.float32r
BF16 = mybir.dt.bfloat16
AX_X = mybir.AxisListType.X
AX_XY = mybir.AxisListType.XY
RMAX = bass.bass_isa.ReduceOp.max
RADD = bass.bass_isa.ReduceOp.add

ROWS = ["L0_gnn_bc", "L0_gnn_g1", "L0_gnn_be1", "L0_gnn_bo", "L0_gnn_g2", "L0_gnn_be2", "L0_gnn_b2",
        "L0_gnn_g3", "L0_gnn_be3", "L2_gnn_bv", "L2_gnn_bo", "L3_gnn_bg0", "L3_gnn_bg1"]
COLS = {"L0_gnn_b1": HC, "L1_gnn_b1": HC, "L1_gnn_g1": HC, "L1_gnn_be1": HC, "L1_gnn_b2": 1, "L1_gnn_g2": 1,
        "L1_gnn_be2": 1, "L2_gnn_bq": 1, "L2_gnn_bk": 1, "L3_gnn_bih": SKIP * GATES, "L3_gnn_bhh": SKIP * GATES}
SQUARES = ["L0_gnn_Wc", "L0_gnn_Wq", "L0_gnn_Wk", "L0_gnn_Wv", "L0_gnn_Wo", "L2_gnn_Wq", "L2_gnn_Wk",
           "L2_gnn_Wv", "L2_gnn_Wo", "L3_gnn_Wg0", "L3_gnn_Wg1"]
NLOADS = 6 + len(ROWS) + len(COLS) + len(SQUARES) + 2

ORDER_A = {
    "SP": [("q0", -2), ("q2", -2), ("q3", -2), ("ldx", 0), ("ldr", -2), ("q1", -1)],
    "PE": [("P1", -2), ("S2", -2), ("xp", 0), ("l1", -5), ("P3", -2), ("h1", 0), ("x2t", -3), ("P2", -2),
           ("S1", -1), ("w1", -3), ("PV", -2), ("S0", -1), ("w2", -3), ("x1t", 0), ("wo", -2), ("qk", 0),
           ("S3", -1), ("agg", -4), ("P0", -1), ("v", 0)],
    "ACT": [("P2", -3), ("w1", -4), ("PV", -3), ("S1", -2), ("x1t", -1), ("S0", -2), ("qk", -1), ("agg", -5),
            ("P0", -2), ("v", -1), ("P1", -2), ("S3", -2), ("xp", 0), ("S2", -2), ("P3", -2), ("x2t", -3),
            ("l1", -5)],
    "DVE": [("w2", -4), ("wo", -3), ("qk", -1), ("n3", -4), ("n2", -3), ("S3", -2), ("S2", -2), ("u4", -4),
            ("rec", -2), ("h1", 0), ("l1", -5), ("n1", 0), ("S1", -1), ("xn", -4), ("S0", -1), ("x1", 0),
            ("PV", -2)],
    "POOL": [("h1", 0), ("u4", -4), ("n1", 0), ("x1", -1), ("xb3", -3), ("xn", -4), ("w2", -3), ("wo", -2),
             ("n3", -3), ("n2", -2), ("PV", -1)]}
ORDER_C = {
    "PE": [("p", -2), ("a0", -4), ("yt", -1), ("pv", -2), ("zt", 0), ("qk", -1), ("x6t", -3), ("wo", -2),
           ("u1", -4), ("s", -1), ("u0", -3), ("g", -2), ("a1", -4), ("v", -1)],
    "ACT": [("pv", -3), ("qk", -2), ("x6t", -4), ("s", -2), ("a1", -5), ("p", -2), ("z", 0), ("yt", -1),
            ("a0", -4)],
    "DVE": [("wo", -3), ("u1", -5), ("s", -2), ("u0", -4), ("g", -3), ("n5", -1), ("v", -2), ("n6", -3),
            ("zt", 0)],
    "POOL": [("zt", 0), ("g", -2), ("n5", -1), ("n6", -2)]}
BODY_E = [("t", 0), ("n", -1), ("c", 1)]


def wait(eng, s, v):
    if not (isinstance(v, int) and v <= 0):
        eng.wait_ge(s, v)


def wait_load(eng, sems, b, par):
    if isinstance(b, int):
        eng.wait_ge(sems[par], 16 * (b // 2 + 1))
    else:
        eng.wait_ge(sems[par], 8 * (b - par) + 16)


def wait_store(eng, sems, b, par):
    if isinstance(b, int):
        wait(eng, sems[par], 16 * (b // 2))
    else:
        eng.wait_ge(sems[par], 8 * (b - par))


def wait_copies(eng, s, b, par):
    if isinstance(b, int):
        wait(eng, s, 16 * COPIES * (b // 2 + 1))
    else:
        eng.wait_ge(s, 8 * COPIES * (b - par) + 16 * COPIES)


class Chain:
    def __init__(self, eng, s):
        self.eng, self.s, self.n = eng, s, 0

    def __call__(self, ins):
        self.n += 1
        ins.then_inc(self.s, 1)

    def sync(self):
        self.eng.wait_ge(self.s, self.n)

    def link(self, ins):
        self(ins)
        self.sync()

    def clear(self):
        if self.n:
            self.sync()
            self.eng.sem_clear(self.s)
        self.n = 0


def bodies(eng, order, steps, total, chain=None):
    order = [(name, off) for name, off in order if name in steps]
    offs = [off for _, off in order]
    first = 2 - min(offs)
    last = total - max(offs)
    first += first % 2
    last -= last % 2

    def body(i, par):
        for name, off in order:
            b = i + off
            if not (isinstance(b, int) and not 0 <= b < total):
                steps[name](b, (par + off) % 2)
        if chain is not None:
            chain.clear()
    for i in range(-max(offs), first):
        body(i, i % 2)
    with eng.Fori(first // 2, last // 2) as k:
        body(k * 2, 0)
        body(k * 2 + 1, 1)
    for i in range(last, total - min(offs)):
        body(i, i % 2)


def build(nc, t, out):
    with ExitStack() as ctx:
        def sb(name, shape, dt=F32, scope=ctx):
            return scope.enter_context(nc.sbuf_tensor(name, shape, dt))

        def sem(name):
            return ctx.enter_context(nc.semaphore(name))

        def sems(prefix, names):
            return {k: sem(f"{prefix}_{k}") for k in names}

        A_nat = sb("A_nat", [P, J, N])
        A_T = sb("A_T", [P, J, N])
        LnT = sb("LnT", [P, J, N])
        AhT = sb("AhT", [P, J, N])
        GT = sb("GT", [P, J, N])
        MaskBias = sb("MaskBias", [P, J, N], BF16)
        ScoreBias = sb("ScoreBias", [P, J, N])
        ident = sb("ident", [P, P])
        eye2 = sb("eye2", [P, J, N])
        ident_b = sb("ident_b", [P, P], BF16)
        ones = sb("ones", [P, P])
        row = {n: sb("row_" + n, [P, D]) for n in ROWS}
        col = {n: sb("col_" + n, [P, k]) for n, k in COLS.items()}
        w = {n: sb("w_" + n, [P, D]) for n in SQUARES}
        W1 = sb("W1", [P, HC * P])
        W2 = sb("W2", [P, HC, D])
        V1 = sb("l1_W1T", [P, HC * P])
        V2 = sb("l1_W2T", [P, HC, D])
        bl = sb("bl", [P, SKIP * GATES])
        scal = sb("scal", [P, 2])
        eps = sb("eps", [P, HC])
        nhalf = sb("nhalf", [P, HC])

        NLN = 7
        bn = [sb(f"bn{k}", [P, J, 6]) for k in range(NLN)]
        mv = [sb(f"mv{k}", [P, J, 2]) for k in range(NLN)]
        ve = [sb(f"ve{k}", [P, J]) for k in range(NLN)]
        rs = [sb(f"rs{k}", [P, J]) for k in range(NLN)]
        bnH = sb("bnH", [P, HC, B, 6])
        mvH, veH, rsH, scH, shH = (sb(n, [P, HC, k]) for n, k in
                                   [("mvH", 2), ("veH", 1), ("rsH", 1), ("scH", 1), ("shH", 1)])
        bnO = sb("bnO", [P, NCH, 6])
        mvO, veO, rsO, scO, shO = (sb(n, [P, k]) for n, k in
                                   [("mvO", 2), ("veO", 1), ("rsO", 1), ("scO", 1), ("shO", 1)])

        X = sb("X", [P, B, J, D])
        sh = ExitStack()
        H = [sb("H0", [P, B * N]), sb("H1", [P, B * N], scope=sh)]
        HT = H[0][:]

        sa = ExitStack()
        with ExitStack() as sp_:
            Sym = sb("Sym", [P, J, N], scope=sp_)
            Pw = [sb(f"Pw{i}", [P, J, N], scope=sp_) for i in range(2)]
            prod = sb("prod", [P, J, N], scope=sp_)
        PTs = [sb(f"PTs{i}", [P, J, HEADS, N], scope=sa) for i in range(2)]
        part = sb("part", [P, 16], scope=sa)
        tot = sb("tot", [P, 16], scope=sa)
        deg = sb("deg", [P, 6 * J], scope=sa)

        def tiles(name, dt=F32):
            return sb(name, [P, J, D], dt, scope=sa)
        Xin = [tiles(f"Xin{i}") for i in range(2)]
        Xres = [tiles(f"Xres{i}") for i in range(2)]
        xpT = sb("xpT", [P, N], scope=sa)
        u1, n1 = tiles("u1"), tiles("n1")
        x1 = [tiles(f"x1_{i}") for i in range(2)]
        x1b = [tiles(f"x1b_{i}") for i in range(2)]
        x1T = sb("x1T", [P, N], scope=sa)
        QK = [sb(f"QK{i}", [P, 4, N], F32R, scope=sa) for i in range(2)]
        Stack = [sb(f"Stack{i}", [P, HEADS, 2, N], F32R, scope=sa) for i in range(2)]
        V = [tiles(f"V{i}") for i in range(2)]
        nmax = sb("nmax", [P, HEADS, J], scope=sa)
        rsum = [sb(f"rsum{i}", [P, HEADS, J], scope=sa) for i in range(2)]
        rinv = sb("rinv", [P, HEADS, J], scope=sa)
        rrep = sb("rrep", [P, J, HEADS, HD], scope=sa)
        Ex = [sb(f"Ex{i}", [P, J, N], scope=sa) for i in range(2)]
        Rs = sb("Rs", [P, N], scope=sa)
        oT = sb("oT", [P, N], scope=sa)
        u2, n2, x2, x2b = tiles("u2"), tiles("n2"), tiles("x2"), tiles("x2b")
        x2T = sb("x2T", [P, N], scope=sa)
        hT = sb("hT", [P, HC, N], scope=sa)
        u3, n3, xb3, u4 = tiles("u3"), tiles("n3"), tiles("xb3"), tiles("u4")
        Xn = [tiles(f"Xn{i}") for i in range(2)]
        aggT = sb("aggT", [P, N], scope=sa)
        sa.close()
        sh.close()

        Wih = sb("Wih", [P, SKIP, GATES, D])
        Whh = sb("Whh", [P, SKIP, GATES, D])
        Gt = [sb(f"Gt{s}", [P, GATES, CH]) for s in range(2)]
        zT = sb("zT", [P, N])
        tile2 = {k: sb("c_" + k, [P, J, D]) for k in ["u5", "R", "u6", "x6", "U0", "U1", "V2", "h"]}
        y = [sb(f"y{i}", [P, J, D]) for i in range(2)]
        yb = [sb(f"yb{i}", [P, J, D]) for i in range(2)]
        yT, aoT, x6T, h1T = (sb(n, [P, N]) for n in ["yT", "aoT", "x6T", "h1T"])
        QK2 = sb("QK2", [P, 2, N])
        Sc = sb("Sc", [P, J, N])
        E2 = sb("E2", [P, J, N])
        PT2 = sb("PT2", [P, J, N])
        nmax2 = sb("nmax2", [P, J])
        rsum2 = [sb(f"rsum2_{i}", [P, J]) for i in range(2)]
        rinv2 = sb("rinv2", [P, J])
        with ExitStack() as sc:
            OT = sb("OT", [P, B * N], scope=sc)
        ct = [sb(f"ct{s}", [P, CH]) for s in range(2)]
        tc = [sb(f"tc{s}", [P, CH]) for s in range(2)]
        ht = [sb(f"ht{s}", [P, CH]) for s in range(2)]
        ig = [sb(f"ig{s}", [P, CH]) for s in range(2)]
        Yo = [sb(f"Yo{i}", [P, J, D]) for i in range(2)]
        u7 = sb("u7", [P, J, D])
        hE = [sb(f"hE{i}", [P, N]) for i in range(2)]

        bank = [ctx.enter_context(nc.psum_tensor(f"bank{i}", [P, 512], F32)) for i in range(8)]
        Sb, Pb, Tb = bank[0:2], bank[2:4], bank[4:6]
        Ob, Hb = bank[6], bank[7]

        s_const, s_eye = sem("s_const"), sem("s_eye")
        s_sq, s_sqe, s_part, s_tot = sem("s_sq"), sem("s_sqe"), sem("s_part"), sem("s_tot")
        s_mats, AHAT, G, POWER, LNT = sem("s_mats"), 1, 2, 3, 4
        xin_in = [sem(f"xin_in{i}") for i in range(2)]
        xres_in = [sem(f"xres_in{i}") for i in range(2)]
        stack_in = [[sem(f"stack_in{h}_{i}") for h in range(HEADS)] for i in range(2)]
        pe = sems("pe", ["xp", "h1", "x1t", "qk", "v", "PV", "wo", "x2t", "w1", "w2", "agg", "l1"])
        pe_S = [sem(f"pe_S{h}") for h in range(HEADS)]
        pe_P = [sem(f"pe_P{h}") for h in range(HEADS)]
        act = sems("act", ["xp", "x1t", "hi", "v", "R", "x2t", "gelu", "agg", "l1"])
        act_exp = [sem(f"act_exp{h}") for h in range(HEADS)]
        act_PT = [sem(f"act_PT{h}") for h in range(HEADS)]
        dve = sems("dve", ["st1", "n1", "x1", "lo", "rinv", "oT", "u2", "st2", "n2", "u3", "st3", "n3",
                           "u4", "st4", "xn", "bnH"])
        dve_max = [sem(f"dve_max{h}") for h in range(HEADS)]
        pool = sems("pool", ["rs1", "f1", "x1b", "rrep", "rs2", "x2", "rs3", "xb3", "f3", "rs4", "save"])
        bnorm, MV_H, RS_H, SC_H, MV_O, RS_O, SC_O = sem("bnorm"), 1, 2, 3, 4, 5, 6
        B_ = sems("B", ["aff", "mm", "ev"])
        pc = sems("pc", ["zt", "yt", "qk", "v", "s", "p", "pv", "wo", "g", "x6t", "u0", "a0", "u1", "a1"])
        ac = sems("ac", ["z", "yt", "qk", "exp", "p", "pv", "x6t", "a0", "a1"])
        dc = sems("dc", ["st5", "y", "V", "max", "R", "st6", "x6", "U0", "U1"])
        gc = sems("gc", ["rs5", "yb", "rs6", "save"])
        L_pe = [sems(f"Lpe{s}", "ifgo") for s in range(2)]
        L_act = [sems(f"Lact{s}", ["f", "g", "o", "tc"]) for s in range(2)]
        L_dve = [sems(f"Ldve{s}", ["c", "h"]) for s in range(2)]
        e_ = sems("e", ["copy", "t", "u", "st", "rs", "y"])
        st_out = [sem(f"st_out{i}") for i in range(2)]
        dchain, gchain = sem("dchain"), sem("gchain")

        UNITS = [(1, 0, 0), (1, 0, 1)] + [(p, st, None) for p in range(2, SKIP + 1) for st in range(p)]
        NU, NF = len(UNITS), sum(st > 0 for _, st, _ in UNITS)

        def windows(g, p, st, half):
            c = HT.rearrange("p (g c) -> p g c", g=NG)[:, g, :]
            if p == 1:
                return c[:, half * CH:(half + 1) * CH]
            if N % p == 0:
                return c.rearrange("p (n q) -> p n q", q=p)[:, :, st]
            c = c.rearrange("p (b n) -> p b n", b=GB)[:, :, 0:N // p * p]
            return c.rearrange("p b (n q) -> p b n q", q=p)[:, :, :, st]

        def width(p):
            return CH if p == 1 else GB * (N // p)

        def shaped(ap, p):
            a = ap[:, 0:width(p)]
            return a if p == 1 or N % p == 0 else a.rearrange("p (b n) -> p b n", b=GB)

        def bcast(ap):
            return ap.unsqueeze(1).broadcast_to([P, J, D])

        def two(bk):
            return bk[:, 0:N].rearrange("p (j d) -> p j d", j=J)

        block = ctx.enter_context(nc.Block())

        @block.sync
        def _(sp):
            loads = [(A_nat[:], t["adj"].rearrange("(j p) n -> p j n", p=P)),
                     (A_T[:], t["adjT"].rearrange("(j p) n -> p j n", p=P)),
                     (W1[:], t["L0_gnn_W1"]), (W2[:], t["L0_gnn_W2"].rearrange("(c p) n -> p c n", p=P)),
                     (V1[:], t["L1_gnn_W1T"]), (V2[:], t["L1_gnn_W2T"].rearrange("(c p) n -> p c n", p=P))]
            loads += [(row[n][:], t[n].partition_broadcast(P)) for n in ROWS]
            loads += [(col[n][:], t[n]) for n in COLS]
            loads += [(w[n][:], t[n]) for n in SQUARES]
            loads += [(scal[:, 0:1], t["L2_gnn_alpha"].partition_broadcast(P)),
                      (scal[:, 1:2], t["L2_gnn_gamma"].partition_broadcast(P))]
            for dst, src in loads:
                sp.dma_start(dst, src).then_inc(s_const, 16)
            assert len(loads) == NLOADS
            sp.wait_ge(s_const, 16 * len(loads))

            def load_x(b, par, dst, s):
                sp.dma_start(dst[par][:], t["x"][b].rearrange("(j p) d -> p j d", p=P)).then_inc(s[par], 16)

            def ldx(b, par):
                wait(sp, pe["xp"], b - 1)
                wait(sp, dve["x1"], b - 1)
                load_x(b, par, Xin, xin_in)

            def ldr(b, par):
                wait(sp, pool["xb3"], b - 1)
                load_x(b, par, Xres, xres_in)

            def q(h):
                def step(b, par):
                    wait(sp, dve["lo"], b + 1)
                    for c in range(COPIES):
                        qpart, kpart = c % 2, c // 2
                        src = QK[par][h * HD:(h + 1) * HD, qpart:2 + kpart + 1:2 + kpart - qpart, :]
                        sp.dma_start(Stack[par][c * HD:(c + 1) * HD, h, :, :].bitcast(F32), src.bitcast(F32))\
                          .then_inc(stack_in[par][h], 16)
                return step

            bodies(sp, ORDER_A["SP"], {"ldx": ldx, "ldr": ldr, "q0": q(0), "q1": q(1), "q2": q(2), "q3": q(3)}, B)

            sp.wait_ge(bnorm, SC_O)
            for p in range(SKIP):
                for dst, src in (Wih, t["L3_gnn_WihT"]), (Whh, t["L3_gnn_WhhT"]):
                    sp.dma_start(dst[:, p, :, :].rearrange("p g d -> p (g d)"), src[p]).then_inc(s_const, 16)

            def n(b, par):
                wait(sp, e_["y"], b + 1)
                sp.dma_start(out[b].rearrange("(j p) d -> p j d", p=P), Yo[par][:]).then_inc(st_out[par], 16)

            bodies(sp, BODY_E, {"n": n}, B)
            for s in st_out:
                sp.wait_ge(s, 16 * B // 2)

        @block.gpsimd
        def _(g):
            g.memset(ident[:], 0.0).then_inc(s_eye, 1)
            g.memset(eye2[:], 0.0).then_inc(s_eye, 1)
            g.memset(ones[:], 1.0).then_inc(s_eye, 1)
            g.memset(nhalf[:], -0.5).then_inc(s_eye, 1)
            g.memset(eps[:], EPS).then_inc(s_eye, 1)
            g.wait_ge(s_eye, 5)
            g.affine_select(out=ident[:], in_=ident[:], compare_op=ALU.not_equal, fill=1.0, base=0,
                            pattern=[[-1, P]], channel_multiplier=1).then_inc(s_eye, 1)
            g.affine_select(out=eye2[:], in_=eye2[:], compare_op=ALU.not_equal, fill=1.0, base=0,
                            pattern=[[P, J], [-1, N]], channel_multiplier=1).then_inc(s_eye, 1)
            chain = Chain(g, gchain)
            g.wait_ge(s_part, 1)
            g.tensor_tensor(deg[:, 4 * J:5 * J], deg[:, 3 * J:4 * J], nhalf[:], ALU.pow).then_inc(s_tot, 1)
            for k, op in enumerate([RMAX] + [RADD] * (SQUARINGS // GROUP) + [RADD]):
                g.wait_ge(s_part, k + 2)
                g.partition_all_reduce(tot[:, 2 * k:2 * k + 2], part[:, 2 * k:2 * k + 2], P, op).then_inc(s_tot, 1)

            def root(out_, var, tmp, n_):
                chain.link(g.tensor_tensor(tmp, var, eps[:, 0:n_], ALU.add))
                return g.tensor_tensor(out_, tmp, nhalf[:, 0:n_], ALU.pow)

            def rstd(k, stats_done, b, done):
                g.wait_ge(stats_done, b + 1)
                root(rs[k][:], mv[k][:, :, 1], ve[k][:], J).then_inc(done, 1)

            def h1(b, par):
                rstd(0, dve["st1"], b, pool["rs1"])

            def pn1(b, par):
                g.wait_ge(dve["n1"], b + 1)
                chain.link(g.tensor_tensor(n1[:], n1[:], bcast(row["L0_gnn_g1"][:]), ALU.mult))
                g.tensor_tensor(n1[:], n1[:], bcast(row["L0_gnn_be1"][:]), ALU.add).then_inc(pool["f1"], 1)

            def px1(b, par):
                g.wait_ge(dve["x1"], b + 1)
                wait(g, dve["u2"], b - 1)
                g.tensor_tensor(x1b[par][:], x1[par][:], bcast(row["L0_gnn_bo"][:]), ALU.add)\
                 .then_inc(pool["x1b"], 1)

            def PV(b, par):
                g.wait_ge(dve["rinv"], b + 1)
                wait(g, pe["PV"], b)
                for h in range(HEADS):
                    e = g.tensor_tensor(rrep[:, :, h, :], rinv[:, h, :].unsqueeze(2).broadcast_to([P, J, HD]),
                                        ones[:, 0:J * HD].rearrange("p (j d) -> p j d", j=J), ALU.mult)
                e.then_inc(pool["rrep"], 1)

            def wo(b, par):
                rstd(1, dve["st2"], b, pool["rs2"])

            def pn2(b, par):
                g.wait_ge(dve["n2"], b + 1)
                chain.link(g.tensor_tensor(n2[:], n2[:], bcast(row["L0_gnn_g2"][:]), ALU.mult))
                wait(g, pe["x2t"], b)
                chain(g.tensor_tensor(x2[:], n2[:], bcast(row["L0_gnn_be2"][:]), ALU.add))
                chain.sync()
                wait(g, dve["u3"], b)
                g.tensor_tensor(x2b[:], x2[:], bcast(row["L0_gnn_b2"][:]), ALU.add).then_inc(pool["x2"], 1)

            def pxb3(b, par):
                wait_load(g, xres_in, b, par)
                wait(g, dve["u4"], b)
                g.tensor_tensor(xb3[:], Xres[par][:], bcast(row["L0_gnn_be3"][:]), ALU.add)\
                 .then_inc(pool["xb3"], 1)

            def w2(b, par):
                rstd(2, dve["st3"], b, pool["rs3"])

            def pn3(b, par):
                g.wait_ge(dve["n3"], b + 1)
                g.tensor_tensor(n3[:], n3[:], bcast(row["L0_gnn_g3"][:]), ALU.mult).then_inc(pool["f3"], 1)

            def pu4(b, par):
                rstd(3, dve["st4"], b, pool["rs4"])

            def pxn(b, par):
                g.wait_ge(dve["xn"], b + 1)
                g.tensor_copy(X[:, b, :, :], Xn[par][:]).then_inc(pool["save"], 1)

            bodies(g, ORDER_A["POOL"], {"h1": h1, "n1": pn1, "x1": px1, "PV": PV, "wo": wo, "n2": pn2, "xb3": pxb3, "w2": w2, "n3": pn3,
                               "u4": pu4, "xn": pxn}, B, chain)

            g.wait_ge(bnorm, MV_H)
            root(rsH[:, :, 0], mvH[:, :, 1], veH[:, :, 0], HC).then_inc(bnorm, 1)
            g.wait_ge(bnorm, MV_O)
            root(rsO[:], mvO[:, 1:2], veO[:], 1).then_inc(bnorm, 1)
            chain.clear()

            def zt(b, par):
                rstd(4, dc["st5"], b, gc["rs5"])

            def n5(b, par):
                g.wait_ge(dc["y"], b + 1)
                wait(g, dc["R"], b - 1)
                g.tensor_tensor(yb[par][:], y[par][:], bcast(row["L2_gnn_bo"][:]), ALU.add).then_inc(gc["yb"], 1)

            def gg(b, par):
                rstd(5, dc["st6"], b, gc["rs6"])

            def n6(b, par):
                g.wait_ge(dc["x6"], b + 1)
                g.tensor_copy(X[:, b, :, :], tile2["x6"][:]).then_inc(gc["save"], 1)

            bodies(g, ORDER_C["POOL"], {"zt": zt, "n5": n5, "g": gg, "n6": n6}, B, chain)

            def et(b, par):
                rstd(6, e_["st"], b, e_["rs"])

            bodies(g, BODY_E, {"t": et}, B, chain)

        @block.scalar
        def _(a):
            a.wait_ge(s_eye, 7)
            a.wait_ge(s_const, 16 * NLOADS)

            def xp(b, par):
                a.wait_ge(pe["xp"], b + 1)
                wait(a, pe["h1"], b)
                a.activation(xpT[:], Hb[:, 0:N], ACT.Copy).then_inc(act["xp"], 1)

            def x1t(b, par):
                a.wait_ge(pe["x1t"], b + 1)
                wait(a, pe["v"], b)
                a.activation(x1T[:], Hb[:, 0:N], ACT.Copy).then_inc(act["x1t"], 1)

            def qk(b, par):
                a.wait_ge(pe["qk"], b + 1)
                for h in range(HEADS):
                    wait_copies(a, stack_in[par][h], b - 2, par)
                a.activation(QK[par][:, 0::2, :], Hb[:].rearrange("p (a n) -> p a n", a=2), ACT.Copy)\
                 .then_inc(act["hi"], 1)

            def v(b, par):
                a.wait_ge(pe["v"], b + 1)
                wait(a, pe["PV"], b - 1)
                a.activation(V[par][:], two(Hb), ACT.Copy).then_inc(act["v"], 1)

            def S(h):
                def step(b, par):
                    a.wait_ge(dve_max[h], b + 1)
                    if h >= 2:
                        a.wait_ge(pe_P[h - 2], b + 1)
                    else:
                        wait(a, pe_P[h + 2], b)
                    wait(a, dve["rinv"], b - 1)
                    for j in range(J):
                        e = a.activation(Ex[h % 2][:, j, :], Sb[h % 2][:, j * N:(j + 1) * N], ACT.Exp,
                                         bias=nmax[:, h, j:j + 1], accum_out=rsum[par][:, h, j:j + 1])
                    e.then_inc(act_exp[h], 1)
                return step

            def Pt(h):
                def step(b, par):
                    a.wait_ge(pe_P[h], b + 1)
                    wait(a, pe["PV"], b - 1)
                    a.activation(PTs[par][:, :, h, :], Pb[h % 2][:].rearrange("p (k n) -> p k n", k=J), ACT.Copy)\
                     .then_inc(act_PT[h], 1)
                return step

            def PV(b, par):
                a.wait_ge(pe["PV"], b + 1)
                wait(a, dve["oT"], b)
                a.activation(Rs[:], Ob[:, N:2 * N], ACT.Copy).then_inc(act["R"], 1)

            def x2t(b, par):
                a.wait_ge(pe["x2t"], b + 1)
                wait(a, pe["w1"], b)
                a.activation(x2T[:], Tb[0][:, 0:N], ACT.Copy).then_inc(act["x2t"], 1)

            def w1(b, par):
                a.wait_ge(pe["w1"], b + 1)
                wait(a, pe["w2"], b)
                for c in range(HC):
                    e = a.activation(hT[:, c, :], Tb[0][:, c * N:(c + 1) * N], ACT.Gelu,
                                     bias=col["L0_gnn_b1"][:, c:c + 1])
                e.then_inc(act["gelu"], 1)

            def agg(b, par):
                a.wait_ge(pe["agg"], b + 1)
                wait(a, pe["l1"], b)
                a.activation(aggT[:], Tb[1][:, 0:N], ACT.Copy).then_inc(act["agg"], 1)

            def l1(b, par):
                a.wait_ge(pe["l1"], b + 1)
                for c in range(HC):
                    e = a.activation(H[c][:].rearrange("p (b n) -> p b n", b=B)[:, b, :],
                                     Tb[1][:, c * N:(c + 1) * N], ACT.Identity, bias=col["L1_gnn_b1"][:, c:c + 1])
                e.then_inc(act["l1"], 1)

            steps = {"xp": xp, "x1t": x1t, "qk": qk, "v": v, "PV": PV, "x2t": x2t, "w1": w1, "agg": agg, "l1": l1}
            for h in range(HEADS):
                steps[f"S{h}"] = S(h)
                steps[f"P{h}"] = Pt(h)
            bodies(a, ORDER_A["ACT"], steps, B)

            a.wait_ge(bnorm, SC_H)

            def aff(c, par):
                for k in range(HC):
                    x = H[k][:].rearrange("p (c n) -> p c n", c=NCH)[:, c, :]
                    e = a.activation(x, x, ACT.Relu, bias=shH[:, k, 0:1], scale=scH[:, k, 0:1])
                e.then_inc(B_["aff"], 1)

            bodies(a, [("aff", 0)], {"aff": aff}, NCH)
            a.wait_ge(bnorm, SC_O)

            def z(b, par):
                wait(a, pc["zt"], b)
                a.activation(zT[:], OT[:].rearrange("p (b n) -> p b n", b=B)[:, b, :], ACT.Identity, bias=shO[:, 0:1],
                             scale=scO[:, 0:1]).then_inc(ac["z"], 1)

            def yt(b, par):
                a.wait_ge(pc["yt"], b + 1)
                wait(a, pc["v"], b)
                a.activation(yT[:], bank[0][:, 0:N], ACT.Copy).then_inc(ac["yt"], 1)

            def qk2(b, par):
                a.wait_ge(pc["qk"], b + 1)
                wait(a, pc["s"], b)
                for k, name in enumerate(["L2_gnn_bq", "L2_gnn_bk"]):
                    e = a.activation(QK2[:, k, :], bank[6][:, k * N:(k + 1) * N], ACT.Identity,
                                     bias=col[name][:, 0:1])
                e.then_inc(ac["qk"], 1)

            def s2(b, par):
                a.wait_ge(dc["max"], b + 1)
                wait(a, pc["p"], b)
                wait(a, dc["R"], b - 1)
                for j in range(J):
                    e = a.activation(E2[:, j, :], Sc[:, j, :], ACT.Exp, bias=nmax2[:, j:j + 1],
                                     accum_out=rsum2[par][:, j:j + 1])
                e.then_inc(ac["exp"], 1)

            def evac(name, free, dst, src, func=ACT.Copy):
                def step(b, par):
                    a.wait_ge(pc[name], b + 1)
                    wait(a, pc[free], b)
                    a.activation(dst, src, func).then_inc(ac[name], 1)
                return step

            def a1(b, par):
                a.wait_ge(pc["a1"], b + 1)
                a.activation(HT.rearrange("p (b n) -> p b n", b=B)[:, b, :], bank[5][:, 0:N], ACT.Relu)\
                 .then_inc(ac["a1"], 1)

            bodies(a, ORDER_C["ACT"], {
                "z": z, "yt": yt, "qk": qk2, "s": s2, "a1": a1,
                "p": evac("p", "pv", PT2[:], bank[1][:].rearrange("p (k n) -> p k n", k=J)),
                "pv": evac("pv", "wo", aoT[:], bank[2][:, 0:N]),
                "x6t": evac("x6t", "u0", x6T[:], bank[4][:, 0:N]),
                "a0": evac("a0", "u1", h1T[:], bank[5][:, 0:N], ACT.Relu)}, B)

            def gates(k, u, s):
                p, st, half = UNITS[u]
                n_ = width(p)
                done = NU * k + u
                nf = NF * k + sum(x[1] > 0 for x in UNITS[:u])
                wait(a, L_dve[s]["h"], done)
                for gi, gate in enumerate("ifgo"):
                    if gate == "f" and st == 0:
                        continue
                    a.wait_ge(L_pe[s][gate], (nf if gate == "f" else done) + 1)
                    e = a.activation(Gt[s][:, gi, 0:n_], bank[4 * s + gi][:, 0:n_],
                                 ACT.Tanh if gate == "g" else ACT.Sigmoid,
                                 bias=bl[:, (p - 1) * GATES + gi:(p - 1) * GATES + gi + 1])
                    if gate != "i":
                        e.then_inc(L_act[s][gate], 1)

            def tanh_c(k, u, s):
                n_ = width(UNITS[u][0])
                a.wait_ge(L_dve[s]["c"], NU * k + u + 1)
                a.activation(tc[s][:, 0:n_], ct[s][:, 0:n_], ACT.Tanh).then_inc(L_act[s]["tc"], 1)

            def pair(k):
                for u in range(NU):
                    for s in range(2):
                        gates(k, u, s)
                        tanh_c(k, u, s)
            pair(0)
            with a.Fori(1, NG // 2) as k:
                pair(k)

            def c(b, par):
                wait(a, e_["t"], b - 1)
                a.activation(hE[par][:], HT.rearrange("p (b n) -> p b n", b=B)[:, b, :], ACT.Copy)\
                 .then_inc(e_["copy"], 1)

            for s in range(2):
                a.wait_ge(L_dve[s]["h"], NU * (NG // 2))
            bodies(a, BODY_E, {"c": c}, B)

        @block.tensor
        def _(pt):
            pt.wait_ge(s_eye, 7)
            for k, m in enumerate([prod, Sym]):
                pt.wait_ge(s_mats, AHAT + k)
                for c in range(J):
                    for j in range(J):
                        mm = pt.transpose(Tb[k][:, c * N + j * P:c * N + (j + 1) * P], m[:, j, c * P:(c + 1) * P],
                                          ident[:])
                mm.then_inc(s_sq, 1)
            pt.wait_ge(s_mats, POWER)
            for k in range(SQUARINGS):
                src = Pw[k % 2]
                if k:
                    pt.wait_ge(s_sqe, k)
                for m in range(J):
                    bk = (Sb, Pb)[k % 2][m]
                    for c in range(J):
                        mm = pt.matmul(bk[:, 0:N], src[:, c, m * P:(m + 1) * P], src[:, c, :],
                                       start=(c == 0), stop=(c == J - 1))
                    mm.then_inc(s_sq, 1)
            pt.wait_ge(s_mats, LNT)

            def product(bk, lhs, rhs, n_=P):
                for j in range(J):
                    mm = pt.matmul(bk[:, j * n_:(j + 1) * n_], lhs(j), rhs, start=True, stop=True)
                return mm

            def turned(bk, m):
                for j in range(J):
                    mm = pt.transpose(bk[:, j * P:(j + 1) * P], m[:, j, :], ident[:])
                return mm

            def cut(m):
                return lambda j: m[:, j * P:(j + 1) * P]

            def summed(bk, lhs, rhs):
                for c in range(J):
                    mm = pt.matmul(bk[:, 0:N], lhs[:, c, :], rhs[:, c, :], start=(c == 0), stop=(c == J - 1))
                return mm

            def xp(b, par):
                wait_load(pt, xin_in, b, par)
                wait(pt, act["v"], b)
                summed(Hb, Xin[par], LnT).then_inc(pe["xp"], 1)

            def h1(b, par):
                pt.wait_ge(act["xp"], b + 1)
                product(Hb, cut(xpT), w["L0_gnn_Wc"][:]).then_inc(pe["h1"], 1)

            def x1t(b, par):
                pt.wait_ge(dve["x1"], b + 1)
                turned(Hb, x1[par]).then_inc(pe["x1t"], 1)

            def qk(b, par):
                pt.wait_ge(act["x1t"], b + 1)
                pt.matmul(Hb[:, 0:N], w["L0_gnn_Wq"][:], x1T[:], start=True, stop=True)
                pt.matmul(Hb[:, N:2 * N], w["L0_gnn_Wk"][:], x1T[:], start=True, stop=True).then_inc(pe["qk"], 1)

            def v(b, par):
                pt.wait_ge(dve["lo"], b + 1)
                product(Hb, cut(x1T), w["L0_gnn_Wv"][:]).then_inc(pe["v"], 1)

            def S(h):
                def step(b, par):
                    wait_copies(pt, stack_in[par][h], b, par)
                    if h >= 2:
                        pt.wait_ge(act_exp[h - 2], b + 1)
                    else:
                        wait(pt, act_exp[h + 2], b)
                    for j in range(J):
                        o = Sb[h % 2][:, j * N:(j + 1) * N]
                        pt.matmul(o, Stack[par][:, h, 0, j * P:(j + 1) * P], Stack[par][:, h, 1, :],
                                  start=True, stop=False)
                        mm = pt.matmul(o, ident_b[:], MaskBias[:, j, :], start=False, stop=True)
                    mm.then_inc(pe_S[h], 1)
                return step

            def Pt(h):
                def step(b, par):
                    pt.wait_ge(act_exp[h], b + 1)
                    if h >= 2:
                        pt.wait_ge(act_PT[h - 2], b + 1)
                    else:
                        wait(pt, act_PT[h + 2], b)
                    for k in range(J):
                        for j in range(J):
                            mm = pt.transpose(Pb[h % 2][:, k * N + j * P:k * N + (j + 1) * P],
                                              Ex[h % 2][:, j, k * P:(k + 1) * P], ident[:])
                    mm.then_inc(pe_P[h], 1)
                return step

            def PV(b, par):
                for h in range(HEADS):
                    pt.wait_ge(act_PT[h], b + 1)
                pt.wait_ge(act["v"], b + 1)
                pt.wait_ge(pool["rrep"], b + 1)
                wait(pt, dve["oT"], b)
                for j in range(J):
                    pt.transpose(Ob[:, N + j * P:N + (j + 1) * P],
                                 rrep[:, j, :, :].rearrange("p h d -> p (h d)"), ident[:])
                for k in range(J):
                    for h in range(HEADS):
                        mm = pt.matmul(Ob[h * HD:(h + 1) * HD, 0:N], V[par][:, k, h * HD:(h + 1) * HD],
                                       PTs[par][:, k, h, :], start=(k == 0), stop=(k == J - 1),
                                       skip_group_check=True)
                mm.then_inc(pe["PV"], 1)

            def wo(b, par):
                pt.wait_ge(dve["oT"], b + 1)
                wait(pt, act["gelu"], b)
                product(Tb[0], cut(oT), w["L0_gnn_Wo"][:]).then_inc(pe["wo"], 1)

            def agg(b, par):
                pt.wait_ge(dve["xn"], b + 1)
                pt.wait_ge(dve["u3"], min(b + 2, B) if isinstance(b, int) else b + 2)
                summed(Tb[1], Xn[par], AhT).then_inc(pe["agg"], 1)

            def x2t(b, par):
                pt.wait_ge(pool["x2"], b + 1)
                turned(Tb[0], x2).then_inc(pe["x2t"], 1)

            def l1(b, par):
                pt.wait_ge(act["agg"], b + 1)
                for c in range(HC):
                    mm = pt.matmul(Tb[1][:, c * N:(c + 1) * N], V1[:, c * P:(c + 1) * P], aggT[:],
                                   start=True, stop=True)
                mm.then_inc(pe["l1"], 1)

            def w1(b, par):
                pt.wait_ge(act["x2t"], b + 1)
                for c in range(HC):
                    mm = pt.matmul(Tb[0][:, c * N:(c + 1) * N], W1[:, c * P:(c + 1) * P], x2T[:],
                                   start=True, stop=True)
                mm.then_inc(pe["w1"], 1)

            def w2(b, par):
                pt.wait_ge(act["gelu"], b + 1)
                wait(pt, act["l1"], b - 1)
                for j in range(J):
                    for c in range(HC):
                        mm = pt.matmul(Tb[1][:, j * P:(j + 1) * P], hT[:, c, j * P:(j + 1) * P], W2[:, c, :],
                                       start=(c == 0), stop=(c == HC - 1))
                mm.then_inc(pe["w2"], 1)

            steps = {"xp": xp, "h1": h1, "x1t": x1t, "qk": qk, "v": v, "PV": PV, "wo": wo, "x2t": x2t, "w1": w1,
                     "w2": w2, "agg": agg, "l1": l1}
            for h in range(HEADS):
                steps[f"S{h}"] = S(h)
                steps[f"P{h}"] = Pt(h)
            bodies(pt, ORDER_A["PE"], steps, B)

            def mm2(c, par):
                pt.wait_ge(B_["aff"], c + 1)
                wait(pt, B_["ev"], c - 1)
                for k in range(HC):
                    mm = pt.matmul(bank[par][:], V2[:, k, :], H[k][:].rearrange("p (c n) -> p c n", c=NCH)[:, c, :],
                                   start=(k == 0), stop=(k == HC - 1))
                mm.then_inc(B_["mm"], 1)

            bodies(pt, [("mm", 0)], {"mm": mm2}, NCH)

            def zt(b, par):
                pt.wait_ge(ac["z"], b + 1)
                wait(pt, ac["yt"], b)
                for j in range(J):
                    mm = pt.transpose(bank[0][:, j * P:(j + 1) * P], zT[:, j * P:(j + 1) * P], ident[:])
                mm.then_inc(pc["zt"], 1)

            def yt(b, par):
                pt.wait_ge(dc["y"], b + 1)
                turned(bank[0], y[par]).then_inc(pc["yt"], 1)

            def qk2(b, par):
                pt.wait_ge(ac["yt"], b + 1)
                wait(pt, ac["qk"], b)
                pt.matmul(bank[6][:, 0:N], w["L2_gnn_Wq"][:], yT[:], start=True, stop=True)
                pt.matmul(bank[6][:, N:2 * N], w["L2_gnn_Wk"][:], yT[:], start=True, stop=True)\
                  .then_inc(pc["qk"], 1)

            def v2(b, par):
                wait(pt, dc["V"], b)
                product(bank[7], cut(yT), w["L2_gnn_Wv"][:]).then_inc(pc["v"], 1)

            def s2(b, par):
                pt.wait_ge(ac["qk"], b + 1)
                wait(pt, ac["p"], b)
                product(bank[1], lambda j: QK2[:, 0, j * P:(j + 1) * P], QK2[:, 1, :], N).then_inc(pc["s"], 1)

            def p2(b, par):
                pt.wait_ge(ac["exp"], b + 1)
                for k in range(J):
                    for j in range(J):
                        mm = pt.transpose(bank[1][:, k * N + j * P:k * N + (j + 1) * P],
                                          E2[:, j, k * P:(k + 1) * P], ident[:])
                mm.then_inc(pc["p"], 1)

            def pv(b, par):
                pt.wait_ge(ac["p"], b + 1)
                pt.wait_ge(dc["V"], b + 1)
                wait(pt, dc["R"], b)
                summed(bank[2], tile2["V2"], PT2).then_inc(pc["pv"], 1)

            def wo2(b, par):
                pt.wait_ge(ac["pv"], b + 1)
                product(bank[2], cut(aoT), w["L2_gnn_Wo"][:]).then_inc(pc["wo"], 1)

            def gg(b, par):
                pt.wait_ge(dc["R"], b + 1)
                wait(pt, ac["x6t"], b)
                for j in range(J):
                    for c in range(J):
                        mm = pt.matmul(bank[4][:, j * P:(j + 1) * P], GT[:, c, j * P:(j + 1) * P],
                                       tile2["R"][:, c, :], start=(c == 0), stop=(c == J - 1))
                mm.then_inc(pc["g"], 1)

            def x6t(b, par):
                pt.wait_ge(dc["x6"], b + 1)
                turned(bank[4], tile2["x6"]).then_inc(pc["x6t"], 1)

            def u0(b, par):
                pt.wait_ge(ac["x6t"], b + 1)
                wait(pt, dc["U1"], b)
                product(bank[3], cut(x6T), w["L3_gnn_Wg0"][:]).then_inc(pc["u0"], 1)

            def a0(b, par):
                pt.wait_ge(dc["U0"], b + 1)
                wait(pt, ac["a1"], b)
                summed(bank[5], tile2["U0"], A_T).then_inc(pc["a0"], 1)

            def u1_(b, par):
                pt.wait_ge(ac["a0"], b + 1)
                product(bank[3], cut(h1T), w["L3_gnn_Wg1"][:]).then_inc(pc["u1"], 1)

            def a1(b, par):
                pt.wait_ge(dc["U1"], b + 1)
                summed(bank[5], tile2["U1"], A_T).then_inc(pc["a1"], 1)

            bodies(pt, ORDER_C["PE"], {"zt": zt, "yt": yt, "qk": qk2, "v": v2, "s": s2, "p": p2, "pv": pv, "wo": wo2,
                                "g": gg, "x6t": x6t, "u0": u0, "a0": a0, "u1": u1_, "a1": a1}, B)

            pt.wait_ge(ac["a1"], B)
            pt.wait_ge(s_const, 16 * (NLOADS + 2 * SKIP))

            def gates(k, u, s):
                p, st, half = UNITS[u]
                g = 2 * k + s
                done = NU * k + u
                nf = NF * k + sum(x[1] > 0 for x in UNITS[:u])
                if st == 0 and p > 1:
                    wait(pt, L_dve[s]["h"], done)

                def mm(gi, gate, wt, rhs, start, stop):
                    return pt.matmul(shaped(bank[4 * s + gi], p), wt[:, p - 1, gi, :], rhs, start=start, stop=stop)
                for gi, gate in enumerate("ifgo"):
                    if gate == "f" and st == 0:
                        continue
                    wait(pt, L_act[s]["g" if gate == "i" else gate], nf if gate == "f" else done)
                    m = mm(gi, gate, Wih, windows(g, p, st, half), True, st == 0)
                    if st == 0:
                        m.then_inc(L_pe[s][gate], 1)
                if st:
                    wait(pt, L_dve[s]["h"], done)
                    for gi, gate in enumerate("ifgo"):
                        mm(gi, gate, Whh, shaped(ht[s], p), False, True).then_inc(L_pe[s][gate], 1)

            def pair(k):
                for u in range(NU):
                    for s in range(2):
                        gates(k, u, s)
            pair(0)
            with pt.Fori(1, NG // 2) as k:
                pair(k)

            def et(b, par):
                pt.wait_ge(e_["copy"], b + 1)
                wait(pt, e_["u"], b - 1)
                for j in range(J):
                    mm = pt.transpose(bank[par][:, j * P:(j + 1) * P], hE[par][:, j * P:(j + 1) * P], ident[:])
                mm.then_inc(e_["t"], 1)

            bodies(pt, BODY_E, {"t": et}, B)

        @block.vector
        def _(d):
            chain = Chain(d, dchain)
            link = chain.link

            d.wait_ge(s_const, 16 * NLOADS)
            d.wait_ge(s_eye, 7)
            chain(d.tensor_reduce(deg[:, 0:J], A_nat[:], AX_X, ALU.add))
            chain(d.tensor_reduce(deg[:, J:2 * J], A_T[:], AX_X, ALU.add))
            link(d.tensor_tensor(prod[:], A_nat[:], eye2[:], ALU.mult))
            link(d.tensor_reduce(deg[:, 2 * J:3 * J], prod[:], AX_X, ALU.add))
            link(d.tensor_tensor(deg[:, 3 * J:4 * J], deg[:, 0:J], deg[:, J:2 * J], ALU.add))
            link(d.tensor_tensor(deg[:, 3 * J:4 * J], deg[:, 3 * J:4 * J], deg[:, 2 * J:3 * J], ALU.subtract))
            d.tensor_scalar(deg[:, 3 * J:4 * J], deg[:, 3 * J:4 * J], 1.0, None, ALU.add).then_inc(s_part, 1)
            chain(d.tensor_scalar(deg[:, 5 * J:6 * J], deg[:, 0:J], 0.0, scal[:, 1:2], ALU.is_gt, ALU.mult))
            chain(d.tensor_copy(ident_b[:], ident[:]))
            chain(d.tensor_scalar(w["L0_gnn_Wq"][:], w["L0_gnn_Wq"][:], HD ** -0.5, None, ALU.mult))
            chain(d.tensor_scalar(w["L2_gnn_Wq"][:], w["L2_gnn_Wq"][:], D ** -0.5, None, ALU.mult))
            chain(d.tensor_scalar(col["L2_gnn_bq"][:], col["L2_gnn_bq"][:], D ** -0.5, None, ALU.mult))
            chain(d.tensor_tensor(bl[:], col["L3_gnn_bih"][:], col["L3_gnn_bhh"][:], ALU.add))
            chain(d.tensor_scalar(MaskBias[:], A_nat[:], 0.0, MASKED, ALU.is_le, ALU.mult))
            link(d.tensor_scalar(ScoreBias[:], A_nat[:], 0.0, MASKED, ALU.is_equal, ALU.mult))
            link(d.scalar_tensor_tensor(ScoreBias[:], A_nat[:], scal[:, 0:1], ScoreBias[:], ALU.mult, ALU.add))
            d.wait_ge(s_tot, 1)
            link(d.tensor_tensor(prod[:], A_nat[:], eye2[:], ALU.add))
            for j in range(J):
                e = d.tensor_scalar(prod[:, j, :], prod[:, j, :], deg[:, 4 * J + j:4 * J + j + 1], None, ALU.mult)
                chain(e) if j < J - 1 else e.then_inc(s_mats, 1)
            link(d.tensor_tensor(Sym[:], A_nat[:], eye2[:], ALU.subtract))
            for j in range(J):
                e = d.scalar_tensor_tensor(Sym[:, j, :], Sym[:, j, :], deg[:, 5 * J + j:5 * J + j + 1],
                                           eye2[:, j, :], ALU.mult, ALU.add)
                chain(e) if j < J - 1 else e.then_inc(s_mats, 1)
            d.wait_ge(s_sq, 1)
            for j in range(J):
                chain(d.tensor_scalar(AhT[:, j, :], Tb[0][:, j * N:(j + 1) * N], deg[:, 4 * J + j:4 * J + j + 1],
                                      None, ALU.mult))
            d.wait_ge(s_sq, 2)
            link(d.tensor_copy(GT[:], Tb[1][:].rearrange("p (j n) -> p j n", j=J)))
            link(d.tensor_tensor(Sym[:], A_nat[:], A_T[:], ALU.add))
            link(d.tensor_scalar(Sym[:], Sym[:], 0.5, None, ALU.mult))
            link(d.tensor_reduce(deg[:, 0:J], Sym[:], AX_X, ALU.add, apply_absolute_value=True))
            link(d.tensor_reduce(part[:, 0:1], deg[:, 0:J], AX_X, ALU.max))
            d.tensor_copy(part[:, 1:2], part[:, 0:1]).then_inc(s_part, 1)
            d.wait_ge(s_tot, 2)
            link(d.tensor_scalar(tot[:, 0:1], tot[:, 0:1], 2.0, 1e-30, ALU.mult, ALU.add))
            link(d.reciprocal(tot[:, 1:2], tot[:, 0:1]))
            link(d.tensor_scalar(prod[:], eye2[:], 0.5, None, ALU.mult))
            d.scalar_tensor_tensor(Pw[0][:], Sym[:], tot[:, 1:2], prod[:], ALU.mult, ALU.add).then_inc(s_mats, 1)

            def trace(k, m, other):
                chain(d.tensor_copy(part[:, 2 * k + 1:2 * k + 2], ones[:, 0:1]))
                link(d.tensor_tensor(prod[:], m[:], other[:], ALU.mult))
                d.tensor_reduce(part[:, 2 * k:2 * k + 1], prod[:], AX_XY, ALU.add).then_inc(s_part, 1)
                d.wait_ge(s_tot, k + 2)

            for k in range(SQUARINGS):
                dst = Pw[(k + 1) % 2]
                r, last = divmod(k + 1, GROUP)
                for m in range(J):
                    d.wait_ge(s_sq, 2 + J * k + m + 1)
                    e = d.tensor_copy(dst[:, m, :], (Sb, Pb)[k % 2][m][:, 0:N])
                    e.then_inc(s_sqe, 1) if last and m == J - 1 else link(e)
                if not last:
                    trace(r, dst, eye2)
                    link(d.reciprocal(tot[:, 2 * r + 1:2 * r + 2], tot[:, 2 * r:2 * r + 1]))
                    d.tensor_scalar(dst[:], dst[:], tot[:, 2 * r + 1:2 * r + 2], None, ALU.mult).then_inc(s_sqe, 1)
            d.wait_ge(s_sqe, SQUARINGS)
            r = SQUARINGS // GROUP + 1
            trace(r, Pw[SQUARINGS % 2], Sym)
            link(d.tensor_scalar(tot[:, 2 * r:2 * r + 1], tot[:, 2 * r:2 * r + 1], 1e-8, None, ALU.add))
            link(d.reciprocal(tot[:, 2 * r + 1:2 * r + 2], tot[:, 2 * r:2 * r + 1]))
            link(d.tensor_scalar(LnT[:], A_T[:], tot[:, 2 * r + 1:2 * r + 2], 2.0, ALU.mult, ALU.mult))
            d.tensor_tensor(LnT[:], LnT[:], eye2[:], ALU.subtract).then_inc(s_mats, 1)
            chain.clear()

            def stats(k, u, done):
                for j in range(J):
                    chain(d.bn_stats(bn[k][:, j, :], u[:, j, :]))
                chain.sync()
                for j in range(J):
                    e = d.bn_aggr(mv[k][:, j, :], bn[k][:, j, :])
                    chain(e) if j < J - 1 else e.then_inc(done, 1)

            def normalise(k, dst, u, b, ready, done):
                d.wait_ge(ready, b + 1)
                for j in range(J):
                    e = d.tensor_scalar(dst[:, j, :], u[:, j, :], mv[k][:, j, 0:1], rs[k][:, j:j + 1],
                                        ALU.subtract, ALU.mult)
                    chain(e) if j < J - 1 else e.then_inc(done, 1)

            def h1(b, par):
                d.wait_ge(pe["h1"], b + 1)
                link(d.tensor_tensor(u1[:], two(Hb), bcast(row["L0_gnn_bc"][:]), ALU.add))
                stats(0, u1, dve["st1"])

            def dn1(b, par):
                wait(d, dve["x1"], b)
                normalise(0, n1, u1, b, pool["rs1"], dve["n1"])

            def dx1(b, par):
                d.wait_ge(pool["f1"], b + 1)
                wait(d, pe["x1t"], b - 1)
                wait(d, pool["x1b"], b - 1)
                d.scalar_tensor_tensor(x1[par][:], n1[:], 0.0, Xin[par][:], ALU.max, ALU.add).then_inc(dve["x1"], 1)

            def qk(b, par):
                d.wait_ge(act["hi"], b + 1)
                d.tensor_tensor(QK[par][:, 1::2, :], Hb[:].rearrange("p (a n) -> p a n", a=2),
                                QK[par][:, 0::2, :].bitcast(F32), ALU.subtract).then_inc(dve["lo"], 1)

            def rec(b, par):
                for h in range(HEADS):
                    d.wait_ge(act_exp[h], b + 1)
                wait(d, pool["rrep"], b)
                d.reciprocal(rinv[:], rsum[par][:]).then_inc(dve["rinv"], 1)

            def S(h):
                def step(b, par):
                    d.wait_ge(pe_S[h], b + 1)
                    wait(d, act_exp[h], b)
                    d.tensor_reduce(nmax[:, h, :], Sb[h % 2][:].rearrange("p (j n) -> p j n", j=J), AX_X, ALU.max,
                                    negate=True).then_inc(dve_max[h], 1)
                return step

            def PV(b, par):
                d.wait_ge(act["R"], b + 1)
                wait(d, pe["wo"], b)
                d.tensor_tensor(oT[:], Ob[:, 0:N], Rs[:], ALU.mult).then_inc(dve["oT"], 1)

            def wo(b, par):
                d.wait_ge(pe["wo"], b + 1)
                d.wait_ge(pool["x1b"], b + 1)
                d.tensor_tensor(u2[:], two(Tb[0]), x1b[par][:], ALU.add).then_inc(dve["u2"], 1)
                d.wait_ge(dve["u2"], b + 1)
                stats(1, u2, dve["st2"])

            def dn2(b, par):
                wait(d, pool["x2"], b)
                normalise(1, n2, u2, b, pool["rs2"], dve["n2"])

            def w2(b, par):
                d.wait_ge(pe["w2"], b + 1)
                d.wait_ge(pool["x2"], b + 1)
                d.tensor_tensor(u3[:], two(Tb[1]), x2b[:], ALU.add).then_inc(dve["u3"], 1)
                d.wait_ge(dve["u3"], b + 1)
                stats(2, u3, dve["st3"])

            def dn3(b, par):
                wait(d, dve["u4"], b)
                normalise(2, n3, u3, b, pool["rs3"], dve["n3"])

            def du4(b, par):
                d.wait_ge(pool["f3"], b + 1)
                d.tensor_tensor(u4[:], n3[:], xb3[:], ALU.add).then_inc(dve["u4"], 1)
                d.wait_ge(dve["u4"], b + 1)
                stats(3, u4, dve["st4"])

            def dxn(b, par):
                wait(d, pe["agg"], b - 1)
                wait(d, pool["save"], b - 1)
                normalise(3, Xn[par], u4, b, pool["rs4"], dve["xn"])

            def l1(b, par):
                d.wait_ge(act["l1"], b + 1)
                for c in range(HC):
                    e = d.bn_stats(bnH[:, c, :, :].rearrange("p b k -> p b k")[:, b, :],
                                   H[c][:].rearrange("p (b n) -> p b n", b=B)[:, b, :])
                e.then_inc(dve["bnH"], 1)

            steps = {"h1": h1, "n1": dn1, "x1": dx1, "qk": qk, "rec": rec, "PV": PV, "wo": wo, "n2": dn2, "w2": w2, "n3": dn3,
                     "u4": du4, "xn": dxn, "l1": l1}
            for h in range(HEADS):
                steps[f"S{h}"] = S(h)
            bodies(d, ORDER_A["DVE"], steps, B, chain)

            def scale_shift(sc_, sh_, mean, rs_, gname, bname, tmp, done):
                link(d.tensor_tensor(sc_, col[gname][:], rs_, ALU.mult))
                link(d.tensor_tensor(tmp, mean, sc_, ALU.mult))
                d.tensor_tensor(sh_, col[bname][:], tmp, ALU.subtract).then_inc(done, 1)

            d.wait_ge(dve["bnH"], B)
            for c in range(HC):
                e = d.bn_aggr(mvH[:, c, :], bnH[:, c, :, :].rearrange("p b k -> p (b k)"))
                chain(e) if c < HC - 1 else e.then_inc(bnorm, 1)
            d.wait_ge(bnorm, RS_H)
            scale_shift(scH[:, :, 0], shH[:, :, 0], mvH[:, :, 0], rsH[:, :, 0], "L1_gnn_g1", "L1_gnn_be1",
                        veH[:, :, 0], bnorm)

            def ev(c, par):
                d.wait_ge(B_["mm"], c + 1)
                o = OT[:].rearrange("p (c n) -> p c n", c=NCH)[:, c, :]
                d.tensor_scalar(o, bank[par][:], col["L1_gnn_b2"][:, 0:1], None, ALU.add).then_inc(B_["ev"], 1)
                d.wait_ge(B_["ev"], c + 1)
                chain(d.bn_stats(bnO[:, c, :], o))

            bodies(d, [("ev", 0)], {"ev": ev}, NCH, chain)
            d.bn_aggr(mvO[:], bnO[:].rearrange("p c k -> p (c k)")).then_inc(bnorm, 1)
            d.wait_ge(bnorm, RS_O)
            scale_shift(scO[:], shO[:], mvO[:, 0:1], rsO[:], "L1_gnn_g2", "L1_gnn_be2", veO[:], bnorm)
            chain.clear()

            T = tile2

            def zt(b, par):
                d.wait_ge(pc["zt"], b + 1)
                link(d.tensor_tensor(T["u5"][:], two(bank[0]), X[:, b, :, :], ALU.add))
                stats(4, T["u5"], dc["st5"])

            def n5(b, par):
                wait(d, pc["yt"], b - 1)
                wait(d, gc["yb"], b - 1)
                normalise(4, y[par], T["u5"], b, gc["rs5"], dc["y"])

            def v2(b, par):
                d.wait_ge(pc["v"], b + 1)
                wait(d, pc["pv"], b)
                d.tensor_tensor(T["V2"][:], two(bank[7]), bcast(row["L2_gnn_bv"][:]), ALU.add).then_inc(dc["V"], 1)

            def s2(b, par):
                d.wait_ge(pc["s"], b + 1)
                wait(d, ac["exp"], b)
                link(d.tensor_tensor(Sc[:], bank[1][:].rearrange("p (j n) -> p j n", j=J), ScoreBias[:], ALU.add))
                d.tensor_reduce(nmax2[:], Sc[:], AX_X, ALU.max, negate=True).then_inc(dc["max"], 1)

            def wo2(b, par):
                d.wait_ge(ac["exp"], b + 1)
                link(d.reciprocal(rinv2[:], rsum2[par][:]))
                d.wait_ge(pc["wo"], b + 1)
                d.wait_ge(gc["yb"], b + 1)
                wait(d, pc["g"], b)
                for j in range(J):
                    e = d.scalar_tensor_tensor(T["R"][:, j, :], bank[2][:, j * P:(j + 1) * P], rinv2[:, j:j + 1],
                                               yb[par][:, j, :], ALU.mult, ALU.add)
                    chain(e) if j < J - 1 else e.then_inc(dc["R"], 1)

            def gg(b, par):
                d.wait_ge(pc["g"], b + 1)
                link(d.tensor_tensor(T["u6"][:], two(bank[4]), y[par][:], ALU.add))
                stats(5, T["u6"], dc["st6"])

            def n6(b, par):
                wait(d, pc["x6t"], b)
                wait(d, gc["save"], b)
                normalise(5, T["x6"], T["u6"], b, gc["rs6"], dc["x6"])

            def U(name, bk, free, dst, bias):
                def step(b, par):
                    d.wait_ge(pc[name], b + 1)
                    wait(d, pc[free], b)
                    d.tensor_tensor(dst[:], two(bk), bcast(row[bias][:]), ALU.add).then_inc(dc[name.upper()], 1)
                return step

            bodies(d, ORDER_C["DVE"], {"zt": zt, "n5": n5, "v": v2, "s": s2, "wo": wo2, "g": gg, "n6": n6,
                               "u0": U("u0", bank[3], "a0", T["U0"], "L3_gnn_bg0"),
                               "u1": U("u1", bank[3], "a1", T["U1"], "L3_gnn_bg1")}, B, chain)

            def cell(k, u, s):
                p, st, half = UNITS[u]
                n_ = width(p)
                done = NU * k + u
                nf = NF * k + sum(x[1] > 0 for x in UNITS[:u])
                G = Gt[s]
                c_ = ct[s][:, 0:n_]
                d.wait_ge(L_act[s]["g"], done + 1)
                if st == 0:
                    d.tensor_tensor(c_, G[:, 0, 0:n_], G[:, 2, 0:n_], ALU.mult).then_inc(L_dve[s]["c"], 1)
                else:
                    chain(d.tensor_tensor(ig[s][:, 0:n_], G[:, 0, 0:n_], G[:, 2, 0:n_], ALU.mult))
                    d.wait_ge(L_act[s]["f"], nf + 1)
                    link(d.tensor_tensor(c_, G[:, 1, 0:n_], c_, ALU.mult))
                    d.tensor_tensor(c_, c_, ig[s][:, 0:n_], ALU.add).then_inc(L_dve[s]["c"], 1)

            def hidden(k, u, s):
                p, st, half = UNITS[u]
                done = NU * k + u
                d.wait_ge(L_act[s]["o"], done + 1)
                d.wait_ge(L_act[s]["tc"], done + 1)
                dst = windows(2 * k + s, p, st, half) if st == p - 1 else shaped(ht[s], p)
                d.tensor_tensor(dst, shaped(Gt[s][:, 3, :], p), shaped(tc[s], p), ALU.mult)\
                 .then_inc(L_dve[s]["h"], 1)

            def pair(k):
                for u in range(NU):
                    for s in range(2):
                        cell(k, u, s)
                        hidden(k, u, s)
                chain.clear()
            pair(0)
            with d.Fori(1, NG // 2) as k:
                pair(k)

            def et(b, par):
                d.wait_ge(e_["t"], b + 1)
                wait(d, e_["y"], b)
                d.tensor_tensor(u7[:], two(bank[par]), X[:, b, :, :], ALU.add).then_inc(e_["u"], 1)
                d.wait_ge(e_["u"], b + 1)
                stats(6, u7, e_["st"])
                wait_store(d, st_out, b, par)
                normalise(6, Yo[par], u7, b, e_["rs"], e_["y"])

            bodies(d, BODY_E, {"t": et}, B, chain)


def kernel(**inputs):
    import numpy as np
    import concourse.bacc as bacc
    from concourse.bass_utils import run_bass_kernel_spmd

    lay = np.ascontiguousarray
    host = {n: lay(inputs[n]) for n in ROWS + SQUARES + ["x", "adj", "L0_gnn_W1", "L0_gnn_W2"]}
    for n, k in COLS.items():
        host[n] = lay(inputs[n].reshape(k, P).T)
    host["adjT"] = lay(inputs["adj"].T)
    host["L1_gnn_W1T"] = lay(inputs["L1_gnn_W1"].T)
    host["L1_gnn_W2T"] = lay(inputs["L1_gnn_W2"].T)
    host["L3_gnn_WihT"] = lay(inputs["L3_gnn_Wih"].transpose(0, 2, 1))
    host["L3_gnn_WhhT"] = lay(inputs["L3_gnn_Whh"].transpose(0, 2, 1))
    for n in ["L2_gnn_alpha", "L2_gnn_gamma"]:
        host[n] = lay(inputs[n]).reshape(1)
    nc = bacc.Bacc("TRN2", target_bir_lowering=False, num_devices=1)
    t = {n: nc.dram_tensor("in_" + n, a.shape, mybir.dt.from_np(a.dtype), kind="ExternalInput").ap()
         for n, a in host.items()}
    out = nc.dram_tensor("out_x", (B, N, D), F32, kind="ExternalOutput").ap()
    build(nc, t, out)
    r = run_bass_kernel_spmd(nc, [{"in_" + n: a for n, a in host.items()}], core_ids=[0])
    return r.results[0]["out_x"]
```

```python
from contextlib import ExitStack

import concourse.bass as bass
from concourse import mybir

P = 128
B = 32
N = 256
J = N // P
D = 128
HEADS = 4
HD = D // HEADS
HC = 2
COPIES = 4
SQUARINGS = 15
NORMALISED = range(2, SQUARINGS, 2)
REDUCTIONS = 2 + len(NORMALISED)
CH = 512
NCH = B * N // CH
GB = 4
GC = GB * N
NG = B // GB
SKIP = 4
GATES = 4
EPS = 1e-5
MASKED = -1e9

ALU = mybir.AluOpType
ACT = mybir.ActivationFunctionType
F32 = mybir.dt.float32
F32R = mybir.dt.float32r
BF16 = mybir.dt.bfloat16
AX_X = mybir.AxisListType.X
AX_XY = mybir.AxisListType.XY
RMAX = bass.bass_isa.ReduceOp.max
RADD = bass.bass_isa.ReduceOp.add

ROWS = ["L0_gnn_bc", "L0_gnn_g1", "L0_gnn_be1", "L0_gnn_bo", "L0_gnn_g2", "L0_gnn_be2", "L0_gnn_b2",
        "L0_gnn_g3", "L0_gnn_be3", "L2_gnn_bo", "L3_gnn_bg1"]
COLS = {"L0_gnn_b1": HC, "L1_gnn_b1": HC, "L1_gnn_g1": HC, "L1_gnn_be1": HC, "L1_gnn_b2": 1, "L1_gnn_g2": 1,
        "L1_gnn_be2": 1, "L2_gnn_bq": 1, "L2_gnn_bk": 1, "L2_gnn_bv": 1, "L3_gnn_bg0": 1,
        "L3_gnn_bih": SKIP * GATES, "L3_gnn_bhh": SKIP * GATES}
SQUARES = ["L0_gnn_Wc", "L0_gnn_Wq", "L0_gnn_Wk", "L0_gnn_Wv", "L0_gnn_Wo", "L2_gnn_Wq", "L2_gnn_Wk",
           "L2_gnn_WvT", "L2_gnn_Wo", "L3_gnn_Wg0", "L3_gnn_Wg1"]
NLOADS = 4 + len(ROWS) + len(COLS) + len(SQUARES) + 2

ORDER_A = {
    "SP": [("ldx", 0), ("ldr", -2), ("q0", -1), ("q1", -1), ("q2", -1), ("q3", -1)],
    "PE": [("x2t", -4), ("h1", -1), ("P2", -3), ("P3", -3), ("w1", -4), ("S0", -2), ("PV", -3), ("S1", -2),
           ("w2", -4), ("wo", -3), ("x1t", -1), ("qk", -1), ("P0", -2), ("agg", -5), ("S2", -2), ("v", -1),
           ("P1", -2), ("S3", -2), ("xp", 0), ("l1", -5)],
    "ACT": [("P1", -2), ("S2", -2), ("xp", 0), ("S3", -2), ("x2t", -3), ("l1", -5), ("P2", -2), ("P3", -2),
            ("w1", -3), ("PV", -2), ("x1t", 0), ("S0", -1), ("qk", 0), ("S1", -1), ("P0", -1), ("agg", -4),
            ("v", 0)],
    "DVE": [("S0", -2), ("S1", -2), ("PV", -3), ("x1", -1), ("w2", -4), ("wo", -3), ("n3", -4), ("qk", -1),
            ("n2", -3), ("S2", -2), ("S3", -2), ("u4", -4), ("rec", -2), ("h1", 0), ("l1", -5), ("xn", -4),
            ("n1", 0)],
    "POOL": [("n3", -4), ("n2", -3), ("x1", -2), ("u4", -4), ("PV", -2), ("h1", 0), ("n1", 0), ("xn", -4),
             ("xb3", -3), ("w2", -3), ("wo", -2)]}
ORDER_C = {
    "PE": [("yt", -1), ("pv", -2), ("qk", -1), ("u1", -4), ("zt", 0), ("v", -1), ("s", -1), ("a1", -4),
           ("g", -2), ("a0", -3), ("p", -1), ("u0", -3)],
    "ACT": [("u0", -4), ("z", 0), ("qk", -1), ("a1", -4), ("s", -1), ("a0", -3), ("p", -1), ("yt", 0)],
    "DVE": [("v", -2), ("u0", -4), ("n6", -3), ("wo", -2), ("u1", -4), ("zt", 0), ("s", -1), ("g", -2),
            ("n5", 0)],
    "POOL": [("n5", -1), ("n6", -3), ("zt", 0), ("g", -2)]}


def wait(eng, s, v):
    if not (isinstance(v, int) and v <= 0):
        eng.wait_ge(s, v)


def wait_load(eng, sems, b, par):
    if isinstance(b, int):
        eng.wait_ge(sems[par], 16 * (b // 2 + 1))
    else:
        eng.wait_ge(sems[par], 8 * (b - par) + 16)


def wait_store(eng, sems, b, par):
    if isinstance(b, int):
        wait(eng, sems[par], 16 * (b // 2))
    else:
        eng.wait_ge(sems[par], 8 * (b - par))


def wait_copies(eng, s, b, par):
    if isinstance(b, int):
        wait(eng, s, 16 * COPIES * (b // 2 + 1))
    else:
        eng.wait_ge(s, 8 * COPIES * (b - par) + 16 * COPIES)


class Chain:
    def __init__(self, eng, s):
        self.eng, self.s, self.n = eng, s, 0

    def __call__(self, ins):
        self.n += 1
        ins.then_inc(self.s, 1)

    def sync(self):
        self.eng.wait_ge(self.s, self.n)

    def link(self, ins):
        self(ins)
        self.sync()

    def clear(self):
        if self.n:
            self.sync()
            self.eng.sem_clear(self.s)
        self.n = 0


def bodies(eng, order, steps, total, chain=None, unroll=4):
    order = [(name, off) for name, off in order if name in steps]
    offs = [off for _, off in order]
    first = 2 - min(offs)
    last = total - max(offs)
    first += -first % unroll
    last -= last % unroll

    def body(i, par):
        for name, off in order:
            b = i + off
            if not (isinstance(b, int) and not 0 <= b < total):
                steps[name](b, (par + off) % 2)
        if chain is not None:
            chain.clear()
    for i in range(-max(offs), first):
        body(i, i % 2)
    with eng.Fori(first // unroll, last // unroll) as k:
        for i in range(unroll):
            body(k * unroll + i, i % 2)
    for i in range(last, total - min(offs)):
        body(i, i % 2)


def build(nc, t, out):
    with ExitStack() as ctx:
        def sb(name, shape, dt=F32, scope=ctx):
            return scope.enter_context(nc.sbuf_tensor(name, shape, dt))

        def sem(name):
            return ctx.enter_context(nc.semaphore(name))

        def sems(prefix, names):
            return {k: sem(f"{prefix}_{k}") for k in names}

        A_nat = sb("A_nat", [P, J, N])
        A_T = sb("A_T", [P, J, N])
        LnT = sb("LnT", [P, J, N])
        AhT = sb("AhT", [P, J, N])
        GT = sb("GT", [P, J, N])
        MaskBias = sb("MaskBias", [P, J, N], BF16)
        ScoreBias = sb("ScoreBias", [P, J, N])
        ident = sb("ident", [P, P])
        ident_b = sb("ident_b", [P, P], BF16)
        ones = sb("ones", [P, P])
        row = {n: sb("row_" + n, [P, D]) for n in ROWS}
        col = {n: sb("col_" + n, [P, k]) for n, k in COLS.items()}
        w = {n: sb("w_" + n, [P, D]) for n in SQUARES}
        W1 = sb("W1", [P, HC * P])
        W2 = sb("W2", [P, HC, D])
        V1 = sb("l1_W1T", [P, HC * P])
        V2 = sb("l1_W2T", [P, HC, D])
        Wvo = sb("Wvo", [P, D])
        bvo = sb("bvo", [P, D])
        AggBias = sb("AggBias", [P, N])
        bl = sb("bl", [P, SKIP * GATES])
        scal = sb("scal", [P, 2])
        eps = sb("eps", [P, 2 * J])
        nhalf = sb("nhalf", [P, 2 * J])

        NLN = 6
        bn = [sb(f"bn{k}", [P, J, 6]) for k in range(NLN)]
        mv = [sb(f"mv{k}", [P, J, 2]) for k in range(NLN)]
        ve = [sb(f"ve{k}", [P, J]) for k in range(NLN)]
        rs = [sb(f"rs{k}", [P, J]) for k in range(NLN)]
        bnE, mvE, veE, rsE = ([[sb(f"{n}{u}{s}", [P, 2 * J] + k) for s in range(2)] for u in range(2)] for n, k in
                              [("bnE", [6]), ("mvE", [2]), ("veE", []), ("rsE", [])])
        scratch = sb("scratch", [P, 1])
        bnH = sb("bnH", [P, HC, B, 6])
        mvH, veH, rsH, scH, shH = (sb(n, [P, HC, k]) for n, k in
                                   [("mvH", 2), ("veH", 1), ("rsH", 1), ("scH", 1), ("shH", 1)])
        bnO = sb("bnO", [P, NCH, 6])
        mvO, veO, rsO, scO, shO = (sb(n, [P, k]) for n, k in
                                   [("mvO", 2), ("veO", 1), ("rsO", 1), ("scO", 1), ("shO", 1)])

        X = sb("X", [P, B, J, D])
        sh = ExitStack()
        H = [sb("H0", [P, B * N]), sb("H1", [P, B * N], scope=sh)]
        HT = H[0][:]

        sa = ExitStack()
        with ExitStack() as sp_:
            eye2 = sb("eye2", [P, J, N], scope=sp_)
            Sym = sb("Sym", [P, J, N], scope=sp_)
            Pw = [sb(f"Pw{i}", [P, J, N], scope=sp_) for i in range(2)]
            Ah = sb("Ah", [P, J, N], scope=sp_)
            G = sb("G", [P, J, N], scope=sp_)
            prod = sb("prod", [P, J, N], scope=sp_)
            BvSpread = sb("BvSpread", [P, P], scope=sp_)
        PTs = [sb(f"PTs{i}", [P, J, HEADS, N], scope=sa) for i in range(2)]
        part = sb("part", [P, REDUCTIONS, 2], scope=sa)
        tot = sb("tot", [P, REDUCTIONS, 2], scope=sa)
        inv = sb("inv", [P, REDUCTIONS, 2], scope=sa)
        deg = sb("deg", [P, 6 * J], scope=sa)

        def tiles(name, dt=F32):
            return sb(name, [P, J, D], dt, scope=sa)
        Xin = [tiles(f"Xin{i}") for i in range(2)]
        Xres = [tiles(f"Xres{i}") for i in range(2)]
        xpT = sb("xpT", [P, N], scope=sa)
        u1, n1 = tiles("u1"), tiles("n1")
        x1 = [tiles(f"x1_{i}") for i in range(2)]
        x1b = [tiles(f"x1b_{i}") for i in range(2)]
        x1T = sb("x1T", [P, N], scope=sa)
        QK = [sb(f"QK{i}", [P, 4, N], F32R, scope=sa) for i in range(2)]
        Stack = [sb(f"Stack{i}", [P, HEADS, 2, N], F32R, scope=sa) for i in range(2)]
        V = [tiles(f"V{i}") for i in range(2)]
        nmax = sb("nmax", [P, HEADS, J], scope=sa)
        rsum = [sb(f"rsum{i}", [P, HEADS, J], scope=sa) for i in range(2)]
        rinv = sb("rinv", [P, HEADS, J], scope=sa)
        rrep = sb("rrep", [P, J, HEADS, HD], scope=sa)
        Ex = [sb(f"Ex{i}", [P, J, N], scope=sa) for i in range(2)]
        Rs = sb("Rs", [P, N], scope=sa)
        oT = sb("oT", [P, N], scope=sa)
        u2, n2, x2, x2b = tiles("u2"), tiles("n2"), tiles("x2"), tiles("x2b")
        x2T = sb("x2T", [P, N], scope=sa)
        hT = sb("hT", [P, HC, N], scope=sa)
        u3, n3, xb3, u4 = tiles("u3"), tiles("n3"), tiles("xb3"), tiles("u4")
        Xn = [tiles(f"Xn{i}") for i in range(2)]
        aggT = sb("aggT", [P, N], scope=sa)
        sa.close()
        sh.close()

        Wih = sb("Wih", [P, SKIP, GATES, D])
        Whh = sb("Whh", [P, SKIP, GATES, D])
        Gt = [sb(f"Gt{s}", [P, GATES, CH]) for s in range(2)]
        zT = sb("zT", [P, N])
        tile2 = {k: sb("c_" + k, [P, J, D]) for k in ["u5", "R", "u6", "U1", "V2"]}
        x6 = [sb(f"x6_{i}", [P, J, D]) for i in range(2)]
        y = [sb(f"y{i}", [P, J, D]) for i in range(2)]
        yb = [sb(f"yb{i}", [P, J, D]) for i in range(2)]
        yT, x6aT, h0T, h1T = (sb(n, [P, N]) for n in ["yT", "x6aT", "h0T", "h1T"])
        QK2 = sb("QK2", [P, 2, N])
        Sc = sb("Sc", [P, J, N])
        E2 = sb("E2", [P, J, N])
        PT2 = sb("PT2", [P, J, N])
        nmax2 = sb("nmax2", [P, J])
        rsum2 = [sb(f"rsum2_{i}", [P, J]) for i in range(2)]
        rinv2 = sb("rinv2", [P, J])
        with ExitStack() as sc:
            OT = sb("OT", [P, B * N], scope=sc)
        ct = [sb(f"ct{s}", [P, CH]) for s in range(2)]
        tc = [sb(f"tc{s}", [P, CH]) for s in range(2)]
        ht = [sb(f"ht{s}", [P, CH]) for s in range(2)]
        ig = [sb(f"ig{s}", [P, CH]) for s in range(2)]
        u7 = [[sb(f"u7_{u}{s}", [P, 2 * J, D]) for s in range(2)] for u in range(2)]
        hE = [sb(f"hE{s}", [P, CH]) for s in range(2)]

        bank = [ctx.enter_context(nc.psum_tensor(f"bank{i}", [P, 512], F32)) for i in range(8)]
        Sb, Pb, Tb = bank[0:2], bank[2:4], bank[4:6]
        Ob, Hb = bank[6], bank[7]

        s_adj, s_const, s_eye = sem("s_adj"), sem("s_const"), sem("s_eye")
        s_sq, s_sqe, s_part, s_tot = sem("s_sq"), sem("s_sqe"), sem("s_part"), sem("s_tot")
        s_mats, POWER, NORM, AHAT, REFINE = sem("s_mats"), 1, {}, 0, 0
        for n_, k in enumerate(NORMALISED):
            NORM[k] = POWER + 1 + n_ + (n_ > 2) + (n_ > 3)
        AHAT, REFINE = NORM[NORMALISED[2]] + 1, NORM[NORMALISED[3]] + 1
        LNT = NORM[NORMALISED[-1]] + 1
        TURN_AH, TURN_G = NORMALISED[3] + 1, NORMALISED[4] + 1
        SQUARED = [[J * k + m + 1 + (k >= TURN_AH) + (k >= TURN_G) for m in range(J)] for k in range(SQUARINGS)]
        xin_in = [sem(f"xin_in{i}") for i in range(2)]
        xres_in = [sem(f"xres_in{i}") for i in range(2)]
        stack_in = [[sem(f"stack_in{h}_{i}") for h in range(HEADS)] for i in range(2)]
        pe = sems("pe", ["xp", "h1", "x1t", "qk", "v", "PV", "wo", "x2t", "w1", "w2", "agg", "l1"])
        pe_S = [sem(f"pe_S{h}") for h in range(HEADS)]
        pe_P = [sem(f"pe_P{h}") for h in range(HEADS)]
        act = sems("act", ["xp", "x1t", "hi", "v", "R", "x2t", "gelu", "agg", "l1"])
        act_exp = [sem(f"act_exp{h}") for h in range(HEADS)]
        act_PT = [sem(f"act_PT{h}") for h in range(HEADS)]
        dve = sems("dve", ["st1", "n1", "x1", "lo", "rinv", "oT", "u2", "st2", "n2", "u3", "st3", "n3",
                           "u4", "st4", "xn", "bnH"])
        dve_max = [sem(f"dve_max{h}") for h in range(HEADS)]
        pool = sems("pool", ["rs1", "f1", "x1b", "rrep", "rs2", "x2", "rs3", "xb3", "f3", "rs4", "save"])
        bnorm, MV_H, RS_H, SC_H, MV_O, RS_O, SC_O = sem("bnorm"), 1, 2, 3, 4, 5, 6
        B_ = sems("B", ["aff", "ev"])
        pc = sems("pc", ["zt", "yt", "qk", "v", "s", "p", "pv", "g", "a0", "u0", "u1", "a1"])
        ac = sems("ac", ["z", "yt", "qk", "exp", "p", "a0", "u0", "a1"])
        dc = sems("dc", ["st5", "y", "V", "max", "R", "st6", "x6", "U0", "U1"])
        gc = sems("gc", ["rs5", "yb", "rs6", "save"])
        L_pe = [sems(f"Lpe{s}", "ifgo") for s in range(2)]
        L_act = [sems(f"Lact{s}", ["f", "g", "o", "tc"]) for s in range(2)]
        L_dve = [sems(f"Ldve{s}", ["c", "h"]) for s in range(2)]
        e_ = sems("e", ["copy", "t", "u", "st", "rs", "y"])
        st_out = [sem(f"st_out{i}") for i in range(2)]
        dchain, gchain = sem("dchain"), sem("gchain")

        UNITS = [(1, 0, 0), (1, 0, 1)] + [(p, st, None) for p in range(2, SKIP + 1) for st in range(p)]
        NU, NF = len(UNITS), sum(st > 0 for _, st, _ in UNITS)

        def windows(g, p, st, half):
            c = HT.rearrange("p (g c) -> p g c", g=NG)[:, g, :]
            if p == 1:
                return c[:, half * CH:(half + 1) * CH]
            if N % p == 0:
                return c.rearrange("p (n q) -> p n q", q=p)[:, :, st]
            c = c.rearrange("p (b n) -> p b n", b=GB)[:, :, 0:N // p * p]
            return c.rearrange("p b (n q) -> p b n q", q=p)[:, :, :, st]

        def width(p):
            return CH if p == 1 else GB * (N // p)

        def shaped(ap, p):
            a = ap[:, 0:width(p)]
            return a if p == 1 or N % p == 0 else a.rearrange("p (b n) -> p b n", b=GB)

        def bcast(ap):
            return ap.unsqueeze(1).broadcast_to([P, J, D])

        def two(bk):
            return bk[:, 0:N].rearrange("p (j d) -> p j d", j=J)

        ITEMS = [(u, s) for u in range(2) for s in range(2)]

        def item(k, u, s):
            return 4 * k - 4 + 2 * u + s

        def two_batches(k, u, s):
            return 4 * k - 4 + 2 * s + u

        block = ctx.enter_context(nc.Block())

        @block.sync
        def _(sp):
            for dst, src in (A_nat, t["adj"]), (A_T, t["adjT"]):
                sp.dma_start(dst[:], src.rearrange("(j p) n -> p j n", p=P)).then_inc(s_adj, 16)
            loads = [(scal[:, 0:1], t["L2_gnn_alpha"].partition_broadcast(P)),
                     (scal[:, 1:2], t["L2_gnn_gamma"].partition_broadcast(P)),
                     (W1[:], t["L0_gnn_W1"]), (W2[:], t["L0_gnn_W2"].rearrange("(c p) n -> p c n", p=P)),
                     (V1[:], t["L1_gnn_W1T"]), (V2[:], t["L1_gnn_W2T"].rearrange("(c p) n -> p c n", p=P))]
            loads += [(row[n][:], t[n].partition_broadcast(P)) for n in ROWS]
            loads += [(col[n][:], t[n]) for n in COLS]
            loads += [(w[n][:], t[n]) for n in SQUARES]
            for dst, src in loads:
                sp.dma_start(dst, src).then_inc(s_const, 16)
            assert len(loads) == NLOADS

            def load_x(b, par, dst, s):
                sp.dma_start(dst[par][:], t["x"][b].rearrange("(j p) d -> p j d", p=P)).then_inc(s[par], 16)

            def ldx(b, par):
                wait(sp, pe["xp"], b - 1)
                wait(sp, dve["x1"], b - 1)
                load_x(b, par, Xin, xin_in)

            def ldr(b, par):
                wait(sp, pool["xb3"], b - 1)
                load_x(b, par, Xres, xres_in)

            def q(h):
                def step(b, par):
                    wait(sp, dve["lo"], b + 1)
                    for c in range(COPIES):
                        qpart, kpart = c % 2, c // 2
                        src = QK[par][h * HD:(h + 1) * HD, qpart:2 + kpart + 1:2 + kpart - qpart, :]
                        sp.dma_start(Stack[par][c * HD:(c + 1) * HD, h, :, :].bitcast(F32), src.bitcast(F32))\
                          .then_inc(stack_in[par][h], 16)
                return step

            bodies(sp, ORDER_A["SP"], {"ldx": ldx, "ldr": ldr, "q0": q(0), "q1": q(1), "q2": q(2), "q3": q(3)}, B)

            sp.wait_ge(s_const, 16 * NLOADS)
            sp.wait_ge(bnorm, SC_O)
            for p in range(SKIP):
                for dst, src in (Wih, t["L3_gnn_WihT"]), (Whh, t["L3_gnn_WhhT"]):
                    sp.dma_start(dst[:, p, :, :].rearrange("p g d -> p (g d)"), src[p]).then_inc(s_const, 16)

            def store(k, u, s):
                sp.wait_ge(e_["y"], item(k, u, s) + 1)
                sp.dma_start(out.rearrange("(q b) (j p) d -> q p (b j) d", b=2, p=P)[two_batches(k, u, s)], u7[u][s][:])\
                  .then_inc(st_out[u], 16)

            def stores(k):
                for u, s in ITEMS:
                    store(k, u, s)
            stores(1)
            with sp.Fori(2, NG // 2) as k:
                stores(k)
            stores(NG // 2)
            for s in st_out:
                sp.wait_ge(s, 16 * B // 4)

        @block.gpsimd
        def _(g):
            g.memset(ident[:], 0.0).then_inc(s_eye, 1)
            g.memset(eye2[:], 0.0).then_inc(s_eye, 1)
            g.memset(ones[:], 1.0).then_inc(s_eye, 1)
            g.memset(nhalf[:], -0.5).then_inc(s_eye, 1)
            g.memset(eps[:], EPS).then_inc(s_eye, 1)
            g.wait_ge(s_eye, 5)
            g.affine_select(out=ident[:], in_=ident[:], compare_op=ALU.not_equal, fill=1.0, base=0,
                            pattern=[[-1, P]], channel_multiplier=1).then_inc(s_eye, 1)
            g.affine_select(out=eye2[:], in_=eye2[:], compare_op=ALU.not_equal, fill=1.0, base=0,
                            pattern=[[P, J], [-1, N]], channel_multiplier=1).then_inc(s_eye, 1)
            chain = Chain(g, gchain)
            for r, op in enumerate([RMAX] + [RADD] * (REDUCTIONS - 1)):
                g.wait_ge(s_part, r + 1 + (r > 1))
                g.partition_all_reduce(tot[:, r, :], part[:, r, :], P, op).then_inc(s_tot, 1)
                if r == 1:
                    g.wait_ge(s_part, r + 2)
                    g.tensor_tensor(deg[:, 4 * J:5 * J], deg[:, 3 * J:4 * J], nhalf[:, 0:J], ALU.pow)\
                     .then_inc(s_tot, 1)

            def root(out_, var, tmp, n_):
                chain.link(g.tensor_tensor(tmp, var, eps[:, 0:n_], ALU.add))
                return g.tensor_tensor(out_, tmp, nhalf[:, 0:n_], ALU.pow)

            def rstd(k, stats_done, b, done):
                g.wait_ge(stats_done, b + 1)
                root(rs[k][:], mv[k][:, :, 1], ve[k][:], J).then_inc(done, 1)

            def h1(b, par):
                rstd(0, dve["st1"], b, pool["rs1"])

            def pn1(b, par):
                g.wait_ge(dve["n1"], b + 1)
                chain.link(g.tensor_tensor(n1[:], n1[:], bcast(row["L0_gnn_g1"][:]), ALU.mult))
                g.tensor_tensor(n1[:], n1[:], bcast(row["L0_gnn_be1"][:]), ALU.add).then_inc(pool["f1"], 1)

            def px1(b, par):
                g.wait_ge(dve["x1"], b + 1)
                wait(g, dve["u2"], b - 1)
                g.tensor_tensor(x1b[par][:], x1[par][:], bcast(row["L0_gnn_bo"][:]), ALU.add)\
                 .then_inc(pool["x1b"], 1)

            def PV(b, par):
                g.wait_ge(dve["rinv"], b + 1)
                wait(g, pe["PV"], b)
                g.tensor_tensor(rrep[:], rinv[:].rearrange("p h j -> p j h").unsqueeze(3)
                                .broadcast_to([P, J, HEADS, HD]),
                                ones[:].rearrange("p (h d) -> p h d", h=HEADS).unsqueeze(1)
                                .broadcast_to([P, J, HEADS, HD]), ALU.mult).then_inc(pool["rrep"], 1)

            def wo(b, par):
                rstd(1, dve["st2"], b, pool["rs2"])

            def pn2(b, par):
                g.wait_ge(dve["n2"], b + 1)
                chain.link(g.tensor_tensor(n2[:], n2[:], bcast(row["L0_gnn_g2"][:]), ALU.mult))
                wait(g, pe["x2t"], b)
                chain(g.tensor_tensor(x2[:], n2[:], bcast(row["L0_gnn_be2"][:]), ALU.add))
                chain.sync()
                wait(g, dve["u3"], b)
                g.tensor_tensor(x2b[:], x2[:], bcast(row["L0_gnn_b2"][:]), ALU.add).then_inc(pool["x2"], 1)

            def pxb3(b, par):
                wait_load(g, xres_in, b, par)
                wait(g, dve["u4"], b)
                g.tensor_tensor(xb3[:], Xres[par][:], bcast(row["L0_gnn_be3"][:]), ALU.add)\
                 .then_inc(pool["xb3"], 1)

            def w2(b, par):
                rstd(2, dve["st3"], b, pool["rs3"])

            def pn3(b, par):
                g.wait_ge(dve["n3"], b + 1)
                g.tensor_tensor(n3[:], n3[:], bcast(row["L0_gnn_g3"][:]), ALU.mult).then_inc(pool["f3"], 1)

            def pu4(b, par):
                rstd(3, dve["st4"], b, pool["rs4"])

            def pxn(b, par):
                g.wait_ge(dve["xn"], b + 1)
                g.tensor_copy(X[:, b, :, :], Xn[par][:]).then_inc(pool["save"], 1)

            bodies(g, ORDER_A["POOL"], {"h1": h1, "n1": pn1, "x1": px1, "PV": PV, "wo": wo, "n2": pn2, "xb3": pxb3, "w2": w2, "n3": pn3,
                               "u4": pu4, "xn": pxn}, B, chain)

            g.wait_ge(bnorm, MV_H)
            root(rsH[:, :, 0], mvH[:, :, 1], veH[:, :, 0], HC).then_inc(bnorm, 1)
            g.wait_ge(bnorm, MV_O)
            root(rsO[:], mvO[:, 1:2], veO[:], 1).then_inc(bnorm, 1)
            chain.clear()

            def zt(b, par):
                rstd(4, dc["st5"], b, gc["rs5"])

            def n5(b, par):
                g.wait_ge(dc["y"], b + 1)
                wait(g, dc["R"], b - 1)
                g.tensor_tensor(yb[par][:], y[par][:], bcast(row["L2_gnn_bo"][:]), ALU.add).then_inc(gc["yb"], 1)

            def gg(b, par):
                rstd(5, dc["st6"], b, gc["rs6"])

            def n6(b, par):
                g.wait_ge(dc["x6"], b + 1)
                g.tensor_copy(X[:, b, :, :], x6[par][:]).then_inc(gc["save"], 1)

            bodies(g, ORDER_C["POOL"], {"zt": zt, "n5": n5, "g": gg, "n6": n6}, B, chain)

            def roots(k):
                for u, s in ITEMS:
                    g.wait_ge(e_["st"], item(k, u, s) + 1)
                    root(rsE[u][s][:], mvE[u][s][:, :, 1], veE[u][s][:], 2 * J).then_inc(e_["rs"], 1)
                chain.clear()
            roots(1)
            with g.Fori(2, NG // 2) as k:
                roots(k)
            roots(NG // 2)

        @block.scalar
        def _(a):
            for k in range(SQUARINGS):
                if k in NORMALISED:
                    a.wait_ge(s_mats, NORM[k])
                for m in range(J):
                    a.wait_ge(s_sq, SQUARED[k][m])
                    scale = inv[:, NORMALISED.index(k) + 1, 1:2] if k in NORMALISED else 1.0
                    e = a.activation(Pw[(k + 1) % 2][:, m, :], (Sb, Pb)[k % 2][m][:, 0:N], ACT.Copy, scale=scale)
                e.then_inc(s_sqe, 1)
            a.wait_ge(s_const, 16 * NLOADS)

            def xp(b, par):
                a.wait_ge(pe["xp"], b + 1)
                wait(a, pe["h1"], b)
                a.activation(xpT[:], Hb[:, 0:N], ACT.Copy).then_inc(act["xp"], 1)

            def x1t(b, par):
                a.wait_ge(pe["x1t"], b + 1)
                wait(a, pe["v"], b)
                a.activation(x1T[:], Hb[:, 0:N], ACT.Copy).then_inc(act["x1t"], 1)

            def qk(b, par):
                a.wait_ge(pe["qk"], b + 1)
                for h in range(HEADS):
                    wait_copies(a, stack_in[par][h], b - 2, par)
                a.activation(QK[par][:, 0::2, :], Hb[:].rearrange("p (a n) -> p a n", a=2), ACT.Copy)\
                 .then_inc(act["hi"], 1)

            def v(b, par):
                a.wait_ge(pe["v"], b + 1)
                wait(a, pe["PV"], b - 1)
                a.activation(V[par][:], two(Hb), ACT.Copy).then_inc(act["v"], 1)

            def S(h):
                def step(b, par):
                    a.wait_ge(dve_max[h], b + 1)
                    if h >= 2:
                        a.wait_ge(pe_P[h - 2], b + 1)
                    else:
                        wait(a, pe_P[h + 2], b)
                    wait(a, dve["rinv"], b - 1)
                    for j in range(J):
                        e = a.activation(Ex[h % 2][:, j, :], Sb[h % 2][:, j * N:(j + 1) * N], ACT.Exp,
                                         bias=nmax[:, h, j:j + 1], accum_out=rsum[par][:, h, j:j + 1])
                    e.then_inc(act_exp[h], 1)
                return step

            def Pt(h):
                def step(b, par):
                    a.wait_ge(pe_P[h], b + 1)
                    wait(a, pe["PV"], b - 1)
                    a.activation(PTs[par][:, :, h, :], Pb[h % 2][:].rearrange("p (k n) -> p k n", k=J), ACT.Copy)\
                     .then_inc(act_PT[h], 1)
                return step

            def PV(b, par):
                a.wait_ge(pe["PV"], b + 1)
                wait(a, dve["oT"], b)
                a.activation(Rs[:], Ob[:, N:2 * N], ACT.Copy).then_inc(act["R"], 1)
                a.activation(scratch[:], eps[:, 0:1], ACT.Exp)

            def x2t(b, par):
                a.wait_ge(pe["x2t"], b + 1)
                wait(a, pe["w1"], b)
                a.activation(x2T[:], Tb[0][:, 0:N], ACT.Copy).then_inc(act["x2t"], 1)

            def w1(b, par):
                a.wait_ge(pe["w1"], b + 1)
                wait(a, pe["w2"], b)
                for c in range(HC):
                    e = a.activation(hT[:, c, :], Tb[0][:, c * N:(c + 1) * N], ACT.Gelu,
                                     bias=col["L0_gnn_b1"][:, c:c + 1])
                e.then_inc(act["gelu"], 1)

            def agg(b, par):
                a.wait_ge(pe["agg"], b + 1)
                wait(a, pe["l1"], b)
                a.activation(aggT[:], Tb[1][:, 0:N], ACT.Copy).then_inc(act["agg"], 1)

            def l1(b, par):
                a.wait_ge(pe["l1"], b + 1)
                for c in range(HC):
                    e = a.activation(H[c][:].rearrange("p (b n) -> p b n", b=B)[:, b, :],
                                     Tb[1][:, c * N:(c + 1) * N], ACT.Identity, bias=col["L1_gnn_b1"][:, c:c + 1])
                e.then_inc(act["l1"], 1)

            steps = {"xp": xp, "x1t": x1t, "qk": qk, "v": v, "PV": PV, "x2t": x2t, "w1": w1, "agg": agg, "l1": l1}
            for h in range(HEADS):
                steps[f"S{h}"] = S(h)
                steps[f"P{h}"] = Pt(h)
            bodies(a, ORDER_A["ACT"], steps, B)

            a.wait_ge(bnorm, SC_H)

            def aff(c, par):
                for k in range(HC):
                    x = H[k][:].rearrange("p (c n) -> p c n", c=NCH)[:, c, :]
                    e = a.activation(x, x, ACT.Relu, bias=shH[:, k, 0:1], scale=scH[:, k, 0:1])
                e.then_inc(B_["aff"], 1)

            for c in range(NCH):
                aff(c, c % 2)
            a.wait_ge(bnorm, SC_O)

            def z(b, par):
                wait(a, pc["zt"], b)
                a.activation(zT[:], OT[:].rearrange("p (b n) -> p b n", b=B)[:, b, :], ACT.Identity, bias=shO[:, 0:1],
                             scale=scO[:, 0:1]).then_inc(ac["z"], 1)

            def yt(b, par):
                a.wait_ge(pc["yt"], b + 1)
                wait(a, pc["v"], b)
                a.activation(yT[:], bank[0][:, 0:N], ACT.Copy).then_inc(ac["yt"], 1)

            def qk2(b, par):
                a.wait_ge(pc["qk"], b + 1)
                wait(a, pc["s"], b)
                for k, name in enumerate(["L2_gnn_bq", "L2_gnn_bk"]):
                    e = a.activation(QK2[:, k, :], bank[6][:, k * N:(k + 1) * N], ACT.Identity,
                                     bias=col[name][:, 0:1])
                e.then_inc(ac["qk"], 1)

            def s2(b, par):
                a.wait_ge(dc["max"], b + 1)
                wait(a, pc["p"], b)
                wait(a, dc["R"], b - 1)
                for j in range(J):
                    e = a.activation(E2[:, j, :], Sc[:, j, :], ACT.Exp, bias=nmax2[:, j:j + 1],
                                     accum_out=rsum2[par][:, j:j + 1])
                e.then_inc(ac["exp"], 1)

            def evac(name, free, dst, src, func=ACT.Copy):
                def step(b, par):
                    a.wait_ge(pc[name], b + 1)
                    wait(a, pc[free], b)
                    a.activation(dst, src, func).then_inc(ac[name], 1)
                return step

            def u0(b, par):
                a.wait_ge(dc["U0"], b + 1)
                wait(a, pc["u1"], b)
                a.activation(h1T[:], h0T[:], ACT.Relu).then_inc(ac["u0"], 1)

            def a1(b, par):
                a.wait_ge(pc["a1"], b + 1)
                a.activation(HT.rearrange("p (b n) -> p b n", b=B)[:, b, :], bank[5][:, 0:N], ACT.Relu)\
                 .then_inc(ac["a1"], 1)

            bodies(a, ORDER_C["ACT"], {
                "z": z, "yt": yt, "qk": qk2, "s": s2, "a1": a1,
                "p": evac("p", "pv", PT2[:], bank[1][:].rearrange("p (k n) -> p k n", k=J)),
                "a0": evac("a0", "u0", x6aT[:], bank[5][:, 0:N]), "u0": u0}, B)

            def gates(k, u, s):
                p, st, half = UNITS[u]
                n_ = width(p)
                done = NU * k + u
                nf = NF * k + sum(x[1] > 0 for x in UNITS[:u])
                wait(a, L_dve[s]["h"], done)
                for gi, gate in enumerate("ifgo"):
                    if gate == "f" and st == 0:
                        continue
                    a.wait_ge(L_pe[s][gate], (nf if gate == "f" else done) + 1)
                    e = a.activation(Gt[s][:, gi, 0:n_], bank[4 * s + gi][:, 0:n_],
                                 ACT.Tanh if gate == "g" else ACT.Sigmoid,
                                 bias=bl[:, (p - 1) * GATES + gi:(p - 1) * GATES + gi + 1])
                    if gate != "i":
                        e.then_inc(L_act[s][gate], 1)

            def tanh_c(k, u, s):
                n_ = width(UNITS[u][0])
                a.wait_ge(L_dve[s]["c"], NU * k + u + 1)
                a.activation(tc[s][:, 0:n_], ct[s][:, 0:n_], ACT.Tanh).then_inc(L_act[s]["tc"], 1)

            def copy(k, u, s):
                a.wait_ge(L_dve[s]["h"], NU * k)
                wait(a, e_["t"], item(k, u, s) - 1)
                a.activation(hE[s][:], windows(2 * k - 2 + s, 1, 0, u), ACT.Copy).then_inc(e_["copy"], 1)

            def pair(k, items=True):
                for u in range(NU):
                    for s in range(2):
                        if items and (u, s) in ITEMS:
                            copy(k, u, s)
                        gates(k, u, s)
                        tanh_c(k, u, s)
            pair(0, False)
            pair(1)
            with a.Fori(2, NG // 2) as k:
                pair(k)
            for u, s in ITEMS:
                copy(NG // 2, u, s)

        @block.tensor
        def _(pt):
            pt.wait_ge(s_eye, 7)

            def turn_matrix(bk, m):
                for c in range(J):
                    for j in range(J):
                        mm = pt.transpose(bk[:, c * N + j * P:c * N + (j + 1) * P], m[:, j, c * P:(c + 1) * P], ident[:])
                mm.then_inc(s_sq, 1)

            def folded_weights():
                pt.matmul(Hb[:, 0:P], w["L2_gnn_WvT"][:], w["L2_gnn_Wo"][:], start=True, stop=True)
                pt.matmul(Hb[:, P:2 * P], BvSpread[:], w["L2_gnn_Wo"][:], start=True, stop=True)
                for c in range(J):
                    pt.matmul(Ob[:, 0:N], ones[:], A_T[:, c, :], start=(c == 0), stop=(c == J - 1))

            pt.wait_ge(s_mats, POWER)
            for k in range(SQUARINGS):
                src = Pw[k % 2]
                if k == TURN_AH:
                    pt.wait_ge(s_mats, AHAT)
                    turn_matrix(Tb[0], Ah)
                if k == TURN_G:
                    pt.wait_ge(s_mats, REFINE)
                    folded_weights()
                    turn_matrix(Tb[1], G)
                if k:
                    pt.wait_ge(s_sqe, k)
                for m in range(J):
                    bk = (Sb, Pb)[k % 2][m]
                    for c in range(J):
                        mm = pt.matmul(bk[:, 0:N], src[:, c, m * P:(m + 1) * P], src[:, c, :],
                                       start=(c == 0), stop=(c == J - 1))
                    mm.then_inc(s_sq, 1)
            pt.wait_ge(s_mats, LNT)

            def product(bk, lhs, rhs, n_=P):
                for j in range(J):
                    mm = pt.matmul(bk[:, j * n_:(j + 1) * n_], lhs(j), rhs, start=True, stop=True)
                return mm

            def turned(bk, m):
                for j in range(J):
                    mm = pt.transpose(bk[:, j * P:(j + 1) * P], m[:, j, :], ident[:])
                return mm

            def cut(m):
                return lambda j: m[:, j * P:(j + 1) * P]

            def summed(bk, lhs, rhs):
                for c in range(J):
                    mm = pt.matmul(bk[:, 0:N], lhs[:, c, :], rhs[:, c, :], start=(c == 0), stop=(c == J - 1))
                return mm

            def xp(b, par):
                wait_load(pt, xin_in, b, par)
                wait(pt, act["v"], b)
                summed(Hb, Xin[par], LnT).then_inc(pe["xp"], 1)

            def h1(b, par):
                pt.wait_ge(act["xp"], b + 1)
                product(Hb, cut(xpT), w["L0_gnn_Wc"][:]).then_inc(pe["h1"], 1)

            def x1t(b, par):
                pt.wait_ge(dve["x1"], b + 1)
                turned(Hb, x1[par]).then_inc(pe["x1t"], 1)

            def qk(b, par):
                pt.wait_ge(act["x1t"], b + 1)
                pt.matmul(Hb[:, 0:N], w["L0_gnn_Wq"][:], x1T[:], start=True, stop=True)
                pt.matmul(Hb[:, N:2 * N], w["L0_gnn_Wk"][:], x1T[:], start=True, stop=True).then_inc(pe["qk"], 1)

            def v(b, par):
                pt.wait_ge(dve["lo"], b + 1)
                product(Hb, cut(x1T), w["L0_gnn_Wv"][:]).then_inc(pe["v"], 1)

            def S(h):
                def step(b, par):
                    wait_copies(pt, stack_in[par][h], b, par)
                    if h >= 2:
                        pt.wait_ge(act_exp[h - 2], b + 1)
                    else:
                        wait(pt, act_exp[h + 2], b)
                    for j in range(J):
                        o = Sb[h % 2][:, j * N:(j + 1) * N]
                        pt.matmul(o, Stack[par][:, h, 0, j * P:(j + 1) * P], Stack[par][:, h, 1, :],
                                  start=True, stop=False)
                        mm = pt.matmul(o, ident_b[:], MaskBias[:, j, :], start=False, stop=True)
                    mm.then_inc(pe_S[h], 1)
                return step

            def Pt(h):
                def step(b, par):
                    pt.wait_ge(act_exp[h], b + 1)
                    if h >= 2:
                        pt.wait_ge(act_PT[h - 2], b + 1)
                    else:
                        wait(pt, act_PT[h + 2], b)
                    for k in range(J):
                        for j in range(J):
                            mm = pt.transpose(Pb[h % 2][:, k * N + j * P:k * N + (j + 1) * P],
                                              Ex[h % 2][:, j, k * P:(k + 1) * P], ident[:])
                    mm.then_inc(pe_P[h], 1)
                return step

            def PV(b, par):
                for h in range(HEADS):
                    pt.wait_ge(act_PT[h], b + 1)
                pt.wait_ge(act["v"], b + 1)
                pt.wait_ge(pool["rrep"], b + 1)
                wait(pt, dve["oT"], b)
                for j in range(J):
                    pt.transpose(Ob[:, N + j * P:N + (j + 1) * P],
                                 rrep[:, j, :, :].rearrange("p h d -> p (h d)"), ident[:])
                for k in range(J):
                    for h in range(HEADS):
                        mm = pt.matmul(Ob[h * HD:(h + 1) * HD, 0:N], V[par][:, k, h * HD:(h + 1) * HD],
                                       PTs[par][:, k, h, :], start=(k == 0), stop=(k == J - 1),
                                       skip_group_check=True)
                mm.then_inc(pe["PV"], 1)

            def wo(b, par):
                pt.wait_ge(dve["oT"], b + 1)
                wait(pt, act["gelu"], b)
                product(Tb[0], cut(oT), w["L0_gnn_Wo"][:]).then_inc(pe["wo"], 1)

            def agg(b, par):
                pt.wait_ge(dve["xn"], b + 1)
                pt.wait_ge(dve["u3"], min(b + 2, B) if isinstance(b, int) else b + 2)
                summed(Tb[1], Xn[par], AhT).then_inc(pe["agg"], 1)

            def x2t(b, par):
                pt.wait_ge(pool["x2"], b + 1)
                turned(Tb[0], x2).then_inc(pe["x2t"], 1)

            def l1(b, par):
                pt.wait_ge(act["agg"], b + 1)
                for c in range(HC):
                    mm = pt.matmul(Tb[1][:, c * N:(c + 1) * N], V1[:, c * P:(c + 1) * P], aggT[:],
                                   start=True, stop=True)
                mm.then_inc(pe["l1"], 1)

            def w1(b, par):
                pt.wait_ge(act["x2t"], b + 1)
                for c in range(HC):
                    mm = pt.matmul(Tb[0][:, c * N:(c + 1) * N], W1[:, c * P:(c + 1) * P], x2T[:],
                                   start=True, stop=True)
                mm.then_inc(pe["w1"], 1)

            def w2(b, par):
                pt.wait_ge(act["gelu"], b + 1)
                wait(pt, act["l1"], b - 1)
                for j in range(J):
                    for c in range(HC):
                        mm = pt.matmul(Tb[1][:, j * P:(j + 1) * P], hT[:, c, j * P:(j + 1) * P], W2[:, c, :],
                                       start=(c == 0), stop=(c == HC - 1))
                mm.then_inc(pe["w2"], 1)

            steps = {"xp": xp, "h1": h1, "x1t": x1t, "qk": qk, "v": v, "PV": PV, "wo": wo, "x2t": x2t, "w1": w1,
                     "w2": w2, "agg": agg, "l1": l1}
            for h in range(HEADS):
                steps[f"S{h}"] = S(h)
                steps[f"P{h}"] = Pt(h)
            bodies(pt, ORDER_A["PE"], steps, B)

            def mm2(c, par):
                pt.wait_ge(B_["aff"], c + 1)
                wait(pt, B_["ev"], c - 1)
                for k in range(HC):
                    mm = pt.matmul(bank[par][:], V2[:, k, :], H[k][:].rearrange("p (c n) -> p c n", c=NCH)[:, c, :],
                                   start=(k == 0), stop=(k == HC - 1))
                mm.then_inc(pe["l1"], 1)

            for c in range(NCH):
                mm2(c, c % 2)

            def zt(b, par):
                pt.wait_ge(ac["z"], b + 1)
                wait(pt, ac["yt"], b)
                for j in range(J):
                    mm = pt.transpose(bank[0][:, j * P:(j + 1) * P], zT[:, j * P:(j + 1) * P], ident[:])
                mm.then_inc(pc["zt"], 1)

            def yt(b, par):
                pt.wait_ge(dc["y"], b + 1)
                turned(bank[0], y[par]).then_inc(pc["yt"], 1)

            def qk2(b, par):
                pt.wait_ge(ac["yt"], b + 1)
                wait(pt, ac["qk"], b)
                pt.matmul(bank[6][:, 0:N], w["L2_gnn_Wq"][:], yT[:], start=True, stop=True)
                pt.matmul(bank[6][:, N:2 * N], w["L2_gnn_Wk"][:], yT[:], start=True, stop=True)\
                  .then_inc(pc["qk"], 1)

            def v2(b, par):
                wait(pt, dc["V"], b)
                product(bank[7], cut(yT), Wvo[:]).then_inc(pc["v"], 1)

            def s2(b, par):
                pt.wait_ge(ac["qk"], b + 1)
                wait(pt, ac["p"], b)
                product(bank[1], lambda j: QK2[:, 0, j * P:(j + 1) * P], QK2[:, 1, :], N).then_inc(pc["s"], 1)

            def p2(b, par):
                pt.wait_ge(ac["exp"], b + 1)
                for k in range(J):
                    for j in range(J):
                        mm = pt.transpose(bank[1][:, k * N + j * P:k * N + (j + 1) * P],
                                          E2[:, j, k * P:(k + 1) * P], ident[:])
                mm.then_inc(pc["p"], 1)

            def pv(b, par):
                pt.wait_ge(ac["p"], b + 1)
                pt.wait_ge(dc["V"], b + 1)
                wait(pt, dc["R"], b)
                for j in range(J):
                    for c in range(J):
                        mm = pt.matmul(bank[2][:, j * P:(j + 1) * P], PT2[:, c, j * P:(j + 1) * P],
                                       tile2["V2"][:, c, :], start=(c == 0), stop=(c == J - 1))
                mm.then_inc(pc["pv"], 1)

            def gg(b, par):
                pt.wait_ge(dc["R"], b + 1)
                wait(pt, dc["st6"], b)
                for j in range(J):
                    for c in range(J):
                        mm = pt.matmul(bank[4][:, j * P:(j + 1) * P], GT[:, c, j * P:(j + 1) * P],
                                       tile2["R"][:, c, :], start=(c == 0), stop=(c == J - 1))
                mm.then_inc(pc["g"], 1)

            def a0(b, par):
                pt.wait_ge(dc["x6"], b + 1)
                wait(pt, ac["a1"], b)
                summed(bank[5], x6[par], A_T).then_inc(pc["a0"], 1)

            def u0(b, par):
                pt.wait_ge(ac["a0"], b + 1)
                wait(pt, dc["U1"], b)
                pt.matmul(bank[3][:, 0:N], w["L3_gnn_Wg0"][:], x6aT[:], start=True, stop=True).then_inc(pc["u0"], 1)

            def u1_(b, par):
                pt.wait_ge(ac["u0"], b + 1)
                product(bank[3], cut(h1T), w["L3_gnn_Wg1"][:]).then_inc(pc["u1"], 1)

            def a1(b, par):
                pt.wait_ge(dc["U1"], b + 1)
                summed(bank[5], tile2["U1"], A_T).then_inc(pc["a1"], 1)

            bodies(pt, ORDER_C["PE"], {"zt": zt, "yt": yt, "qk": qk2, "v": v2, "s": s2, "p": p2, "pv": pv,
                                "g": gg, "u0": u0, "a0": a0, "u1": u1_, "a1": a1}, B)

            pt.wait_ge(ac["a1"], B)
            pt.wait_ge(s_const, 16 * (NLOADS + 2 * SKIP))

            def gates(k, u, s):
                p, st, half = UNITS[u]
                g = 2 * k + s
                done = NU * k + u
                nf = NF * k + sum(x[1] > 0 for x in UNITS[:u])
                if st == 0 and p > 1:
                    wait(pt, L_dve[s]["h"], done)

                def mm(gi, gate, wt, rhs, start, stop):
                    return pt.matmul(shaped(bank[4 * s + gi], p), wt[:, p - 1, gi, :], rhs, start=start, stop=stop)
                for gi, gate in enumerate("ifgo"):
                    if gate == "f" and st == 0:
                        continue
                    wait(pt, L_act[s]["g" if gate == "i" else gate], nf if gate == "f" else done)
                    m = mm(gi, gate, Wih, windows(g, p, st, half), True, st == 0)
                    if st == 0:
                        m.then_inc(L_pe[s][gate], 1)
                if st:
                    wait(pt, L_dve[s]["h"], done)
                    for gi, gate in enumerate("ifgo"):
                        mm(gi, gate, Whh, shaped(ht[s], p), False, True).then_inc(L_pe[s][gate], 1)

            def turn(k, u, s):
                pt.wait_ge(e_["copy"], item(k, u, s) + 1)
                pt.wait_ge(L_act[s]["f"], NF * k)
                wait(pt, e_["u"], item(k, u, s) - 1)
                for j in range(2 * J):
                    mm = pt.transpose(bank[4 * s + 1][:, j * P:(j + 1) * P], hE[s][:, j * P:(j + 1) * P], ident[:])
                mm.then_inc(e_["t"], 1)

            def pair(k, items=True):
                for u in range(NU):
                    for s in range(2):
                        if items and u == UNITS.index((2, 1, None)):
                            pt.wait_ge(e_["u"], item(k, 1, s) + 1)
                        gates(k, u, s)
                        if items and (u, s) in ITEMS:
                            turn(k, u, s)
            pair(0, False)
            pair(1)
            with pt.Fori(2, NG // 2) as k:
                pair(k)
            for u, s in ITEMS:
                turn(NG // 2, u, s)

        @block.vector
        def _(d):
            chain = Chain(d, dchain)
            link = chain.link

            d.wait_ge(s_adj, 16 * 2)
            chain(d.memset(part[:], 1.0))
            link(d.tensor_tensor(Sym[:], A_nat[:], A_T[:], ALU.add))
            link(d.tensor_scalar(Sym[:], Sym[:], 0.5, None, ALU.mult))
            link(d.tensor_reduce(deg[:, 0:J], Sym[:], AX_X, ALU.add, apply_absolute_value=True))
            d.tensor_reduce(part[:, 0, 0:1], deg[:, 0:J], AX_X, ALU.max).then_inc(s_part, 1)
            d.wait_ge(s_eye, 7)
            link(d.tensor_scalar(prod[:], eye2[:], 0.5, None, ALU.mult))
            d.wait_ge(s_tot, 1)
            link(d.tensor_scalar(tot[:, 0, 0:1], tot[:, 0, 0:1], 2.0, 1e-30, ALU.mult, ALU.add))
            link(d.reciprocal(inv[:, 0, 0:1], tot[:, 0, 0:1]))
            d.scalar_tensor_tensor(Pw[0][:], Sym[:], inv[:, 0, 0:1], prod[:], ALU.mult, ALU.add).then_inc(s_mats, 1)

            def diagonal(dst, m):
                for j in range(J):
                    e = d.tensor_tensor(prod[:, 0, j * P:(j + 1) * P], m[:, j, j * P:(j + 1) * P], ident[:], ALU.mult)
                    chain(e) if j < J - 1 else link(e)
                return d.tensor_reduce(dst, prod[:, 0, :], AX_X, ALU.add)

            def degrees():
                chain(d.tensor_reduce(deg[:, 0:J], A_nat[:], AX_X, ALU.add))
                chain(d.tensor_reduce(deg[:, J:2 * J], A_T[:], AX_X, ALU.add))
                link(d.tensor_tensor(prod[:], A_nat[:], eye2[:], ALU.mult))
                link(d.tensor_reduce(deg[:, 2 * J:3 * J], prod[:], AX_X, ALU.add))
                link(d.tensor_tensor(deg[:, 3 * J:4 * J], deg[:, 0:J], deg[:, J:2 * J], ALU.add))
                link(d.tensor_tensor(deg[:, 3 * J:4 * J], deg[:, 3 * J:4 * J], deg[:, 2 * J:3 * J], ALU.subtract))
                d.tensor_scalar(deg[:, 3 * J:4 * J], deg[:, 3 * J:4 * J], 1.0, None, ALU.add).then_inc(s_part, 1)

            def masks():
                d.wait_ge(s_const, 16 * NLOADS)
                chain(d.tensor_copy(ident_b[:], ident[:]))
                chain(d.tensor_scalar(BvSpread[:], ones[:], col["L2_gnn_bv"][:, 0:1], None, ALU.mult))
                chain(d.tensor_scalar(w["L0_gnn_Wq"][:], w["L0_gnn_Wq"][:], HD ** -0.5, None, ALU.mult))
                chain(d.tensor_scalar(w["L2_gnn_Wq"][:], w["L2_gnn_Wq"][:], D ** -0.5, None, ALU.mult))
                chain(d.tensor_scalar(col["L2_gnn_bq"][:], col["L2_gnn_bq"][:], D ** -0.5, None, ALU.mult))
                chain(d.tensor_tensor(bl[:], col["L3_gnn_bih"][:], col["L3_gnn_bhh"][:], ALU.add))
                chain(d.tensor_scalar(MaskBias[:], A_nat[:], 0.0, MASKED, ALU.is_le, ALU.mult))
                link(d.tensor_scalar(ScoreBias[:], A_nat[:], 0.0, MASKED, ALU.is_equal, ALU.mult))
                link(d.scalar_tensor_tensor(ScoreBias[:], A_nat[:], scal[:, 0:1], ScoreBias[:], ALU.mult, ALU.add))

            def normalised_adjacency():
                d.wait_ge(s_tot, 3)
                link(d.tensor_tensor(Ah[:], A_nat[:], eye2[:], ALU.add))
                for j in range(J):
                    e = d.tensor_scalar(Ah[:, j, :], Ah[:, j, :], deg[:, 4 * J + j:4 * J + j + 1], None, ALU.mult)
                    chain(e) if j < J - 1 else e.then_inc(s_mats, 1)

            def refinement():
                chain(d.tensor_scalar(deg[:, 5 * J:6 * J], deg[:, 0:J], 0.0, scal[:, 1:2], ALU.is_gt, ALU.mult))
                link(d.tensor_tensor(G[:], A_nat[:], eye2[:], ALU.subtract))
                for j in range(J):
                    e = d.scalar_tensor_tensor(G[:, j, :], G[:, j, :], deg[:, 5 * J + j:5 * J + j + 1],
                                               eye2[:, j, :], ALU.mult, ALU.add)
                    chain(e) if j < J - 1 else e.then_inc(s_mats, 1)

            def scaled_transpose():
                d.wait_ge(s_sq, SQUARED[TURN_AH][0] - 1)
                for j in range(J):
                    chain(d.tensor_scalar(AhT[:, j, :], Tb[0][:, j * N:(j + 1) * N],
                                          deg[:, 4 * J + j:4 * J + j + 1], None, ALU.mult))

            def transposed_refinement():
                d.wait_ge(s_sq, SQUARED[TURN_G][0] - 1)
                chain(d.tensor_copy(GT[:], Tb[1][:].rearrange("p (j n) -> p j n", j=J)))
                chain(d.tensor_copy(Wvo[:], Hb[:, 0:P]))
                chain(d.tensor_copy(bvo[:], Hb[:, P:2 * P]))
                chain(d.tensor_scalar(AggBias[:], Ob[:, 0:N], col["L3_gnn_bg0"][:, 0:1], None, ALU.mult))

            others = [degrees, masks, normalised_adjacency, refinement, scaled_transpose, transposed_refinement]
            for n_, k in enumerate(NORMALISED):
                r = n_ + 1
                d.wait_ge(s_sqe, k)
                diagonal(part[:, r, 0:1], Pw[k % 2]).then_inc(s_part, 1)
                d.wait_ge(s_tot, r + 1 + (r > 1))
                link(d.reciprocal(inv[:, r, 0:1], tot[:, r, 0:1]))
                d.tensor_tensor(inv[:, r, 1:2], inv[:, r, 0:1], inv[:, r, 0:1], ALU.mult).then_inc(s_mats, 1)
                if n_ < len(others):
                    chain.sync()
                    others[n_]()
                    chain.sync()
            d.wait_ge(s_sqe, SQUARINGS)
            r = REDUCTIONS - 1
            link(diagonal(part[:, r, 1:2], Pw[SQUARINGS % 2]))
            link(d.tensor_tensor(prod[:], Pw[SQUARINGS % 2][:], Sym[:], ALU.mult))
            d.tensor_reduce(part[:, r, 0:1], prod[:], AX_XY, ALU.add).then_inc(s_part, 1)
            d.wait_ge(s_tot, r + 2)
            link(d.reciprocal(inv[:, r, 1:2], tot[:, r, 1:2]))
            link(d.tensor_tensor(tot[:, r, 0:1], tot[:, r, 0:1], inv[:, r, 1:2], ALU.mult))
            link(d.tensor_scalar(tot[:, r, 0:1], tot[:, r, 0:1], 1e-8, None, ALU.add))
            link(d.reciprocal(inv[:, r, 0:1], tot[:, r, 0:1]))
            link(d.tensor_scalar(LnT[:], A_T[:], inv[:, r, 0:1], 2.0, ALU.mult, ALU.mult))
            d.tensor_tensor(LnT[:], LnT[:], eye2[:], ALU.subtract).then_inc(s_mats, 1)
            chain.clear()

            def stats(k, u, done):
                for j in range(J):
                    chain(d.bn_stats(bn[k][:, j, :], u[:, j, :]))
                chain.sync()
                for j in range(J):
                    e = d.bn_aggr(mv[k][:, j, :], bn[k][:, j, :])
                    chain(e) if j < J - 1 else e.then_inc(done, 1)

            def normalise(k, dst, u, b, ready, done):
                d.wait_ge(ready, b + 1)
                for j in range(J):
                    e = d.tensor_scalar(dst[:, j, :], u[:, j, :], mv[k][:, j, 0:1], rs[k][:, j:j + 1],
                                        ALU.subtract, ALU.mult)
                    chain(e) if j < J - 1 else e.then_inc(done, 1)

            def h1(b, par):
                d.wait_ge(pe["h1"], b + 1)
                link(d.tensor_tensor(u1[:], two(Hb), bcast(row["L0_gnn_bc"][:]), ALU.add))
                stats(0, u1, dve["st1"])

            def dn1(b, par):
                wait(d, dve["x1"], b)
                normalise(0, n1, u1, b, pool["rs1"], dve["n1"])

            def dx1(b, par):
                d.wait_ge(pool["f1"], b + 1)
                wait(d, pe["x1t"], b - 1)
                wait(d, pool["x1b"], b - 1)
                d.scalar_tensor_tensor(x1[par][:], n1[:], 0.0, Xin[par][:], ALU.max, ALU.add).then_inc(dve["x1"], 1)

            def qk(b, par):
                d.wait_ge(act["hi"], b + 1)
                d.tensor_tensor(QK[par][:, 1::2, :], Hb[:].rearrange("p (a n) -> p a n", a=2),
                                QK[par][:, 0::2, :].bitcast(F32), ALU.subtract).then_inc(dve["lo"], 1)

            def rec(b, par):
                for h in range(HEADS):
                    d.wait_ge(act_exp[h], b + 1)
                wait(d, pool["rrep"], b)
                d.reciprocal(rinv[:], rsum[par][:]).then_inc(dve["rinv"], 1)

            def S(h):
                def step(b, par):
                    d.wait_ge(pe_S[h], b + 1)
                    wait(d, act_exp[h], b)
                    d.tensor_reduce(nmax[:, h, :], Sb[h % 2][:].rearrange("p (j n) -> p j n", j=J), AX_X, ALU.max,
                                    negate=True).then_inc(dve_max[h], 1)
                return step

            def PV(b, par):
                d.wait_ge(act["R"], b + 1)
                wait(d, pe["wo"], b)
                d.tensor_tensor(oT[:], Ob[:, 0:N], Rs[:], ALU.mult).then_inc(dve["oT"], 1)

            def wo(b, par):
                d.wait_ge(pe["wo"], b + 1)
                d.wait_ge(pool["x1b"], b + 1)
                d.tensor_tensor(u2[:], two(Tb[0]), x1b[par][:], ALU.add).then_inc(dve["u2"], 1)
                d.wait_ge(dve["u2"], b + 1)
                stats(1, u2, dve["st2"])

            def dn2(b, par):
                wait(d, pool["x2"], b)
                normalise(1, n2, u2, b, pool["rs2"], dve["n2"])

            def w2(b, par):
                d.wait_ge(pe["w2"], b + 1)
                d.wait_ge(pool["x2"], b + 1)
                d.tensor_tensor(u3[:], two(Tb[1]), x2b[:], ALU.add).then_inc(dve["u3"], 1)
                d.wait_ge(dve["u3"], b + 1)
                stats(2, u3, dve["st3"])

            def dn3(b, par):
                wait(d, dve["u4"], b)
                normalise(2, n3, u3, b, pool["rs3"], dve["n3"])

            def du4(b, par):
                d.wait_ge(pool["f3"], b + 1)
                d.tensor_tensor(u4[:], n3[:], xb3[:], ALU.add).then_inc(dve["u4"], 1)
                d.wait_ge(dve["u4"], b + 1)
                stats(3, u4, dve["st4"])

            def dxn(b, par):
                wait(d, pe["agg"], b - 1)
                wait(d, pool["save"], b - 1)
                normalise(3, Xn[par], u4, b, pool["rs4"], dve["xn"])

            def l1(b, par):
                d.wait_ge(act["l1"], b + 1)
                for c in range(HC):
                    e = d.bn_stats(bnH[:, c, :, :].rearrange("p b k -> p b k")[:, b, :],
                                   H[c][:].rearrange("p (b n) -> p b n", b=B)[:, b, :])
                e.then_inc(dve["bnH"], 1)

            steps = {"h1": h1, "n1": dn1, "x1": dx1, "qk": qk, "rec": rec, "PV": PV, "wo": wo, "n2": dn2, "w2": w2, "n3": dn3,
                     "u4": du4, "xn": dxn, "l1": l1}
            for h in range(HEADS):
                steps[f"S{h}"] = S(h)
            bodies(d, ORDER_A["DVE"], steps, B, chain)

            def scale_shift(sc_, sh_, mean, rs_, gname, bname, tmp, done):
                link(d.tensor_tensor(sc_, col[gname][:], rs_, ALU.mult))
                link(d.tensor_tensor(tmp, mean, sc_, ALU.mult))
                d.tensor_tensor(sh_, col[bname][:], tmp, ALU.subtract).then_inc(done, 1)

            d.wait_ge(dve["bnH"], B)
            for c in range(HC):
                e = d.bn_aggr(mvH[:, c, :], bnH[:, c, :, :].rearrange("p b k -> p (b k)"))
                chain(e) if c < HC - 1 else e.then_inc(bnorm, 1)
            d.wait_ge(bnorm, RS_H)
            scale_shift(scH[:, :, 0], shH[:, :, 0], mvH[:, :, 0], rsH[:, :, 0], "L1_gnn_g1", "L1_gnn_be1",
                        veH[:, :, 0], bnorm)

            def ev(c, par):
                d.wait_ge(pe["l1"], B + c + 1)
                o = OT[:].rearrange("p (c n) -> p c n", c=NCH)[:, c, :]
                d.tensor_scalar(o, bank[par][:], col["L1_gnn_b2"][:, 0:1], None, ALU.add).then_inc(B_["ev"], 1)
                d.wait_ge(B_["ev"], c + 1)
                chain(d.bn_stats(bnO[:, c, :], o))

            for c in range(NCH):
                ev(c, c % 2)
            chain.sync()
            d.bn_aggr(mvO[:], bnO[:].rearrange("p c k -> p (c k)")).then_inc(bnorm, 1)
            d.wait_ge(bnorm, RS_O)
            scale_shift(scO[:], shO[:], mvO[:, 0:1], rsO[:], "L1_gnn_g2", "L1_gnn_be2", veO[:], bnorm)
            chain.clear()

            T = tile2

            def zt(b, par):
                d.wait_ge(pc["zt"], b + 1)
                link(d.tensor_tensor(T["u5"][:], two(bank[0]), X[:, b, :, :], ALU.add))
                stats(4, T["u5"], dc["st5"])

            def n5(b, par):
                wait(d, pc["yt"], b - 1)
                wait(d, gc["yb"], b - 1)
                normalise(4, y[par], T["u5"], b, gc["rs5"], dc["y"])

            def v2(b, par):
                d.wait_ge(pc["v"], b + 1)
                wait(d, pc["pv"], b)
                d.tensor_tensor(T["V2"][:], two(bank[7]), bcast(bvo[:]), ALU.add).then_inc(dc["V"], 1)

            def s2(b, par):
                d.wait_ge(pc["s"], b + 1)
                wait(d, ac["exp"], b)
                link(d.tensor_tensor(Sc[:], bank[1][:].rearrange("p (j n) -> p j n", j=J), ScoreBias[:], ALU.add))
                d.tensor_reduce(nmax2[:], Sc[:], AX_X, ALU.max, negate=True).then_inc(dc["max"], 1)

            def wo2(b, par):
                d.wait_ge(ac["exp"], b + 1)
                link(d.reciprocal(rinv2[:], rsum2[par][:]))
                d.wait_ge(pc["pv"], b + 1)
                d.wait_ge(gc["yb"], b + 1)
                wait(d, pc["g"], b)
                for j in range(J):
                    e = d.scalar_tensor_tensor(T["R"][:, j, :], bank[2][:, j * P:(j + 1) * P], rinv2[:, j:j + 1],
                                               yb[par][:, j, :], ALU.mult, ALU.add)
                    chain(e) if j < J - 1 else e.then_inc(dc["R"], 1)

            def gg(b, par):
                d.wait_ge(pc["g"], b + 1)
                link(d.tensor_tensor(T["u6"][:], two(bank[4]), y[par][:], ALU.add))
                stats(5, T["u6"], dc["st6"])

            def n6(b, par):
                wait(d, pc["a0"], b - 1)
                wait(d, gc["save"], b - 1)
                normalise(5, x6[par], T["u6"], b, gc["rs6"], dc["x6"])

            def u0(b, par):
                d.wait_ge(pc["u0"], b + 1)
                wait(d, ac["u0"], b)
                d.tensor_tensor(h0T[:], bank[3][:, 0:N], AggBias[:], ALU.add).then_inc(dc["U0"], 1)

            def u1_(b, par):
                d.wait_ge(pc["u1"], b + 1)
                wait(d, pc["a1"], b)
                d.tensor_tensor(T["U1"][:], two(bank[3]), bcast(row["L3_gnn_bg1"][:]), ALU.add)\
                 .then_inc(dc["U1"], 1)

            bodies(d, ORDER_C["DVE"], {"zt": zt, "n5": n5, "v": v2, "s": s2, "wo": wo2, "g": gg, "n6": n6, "u0": u0,
                                       "u1": u1_}, B, chain)

            def cell(k, u, s):
                p, st, half = UNITS[u]
                n_ = width(p)
                done = NU * k + u
                nf = NF * k + sum(x[1] > 0 for x in UNITS[:u])
                G = Gt[s]
                c_ = ct[s][:, 0:n_]
                d.wait_ge(L_act[s]["g"], done + 1)
                if st == 0:
                    d.tensor_tensor(c_, G[:, 0, 0:n_], G[:, 2, 0:n_], ALU.mult).then_inc(L_dve[s]["c"], 1)
                else:
                    chain(d.tensor_tensor(ig[s][:, 0:n_], G[:, 0, 0:n_], G[:, 2, 0:n_], ALU.mult))
                    d.wait_ge(L_act[s]["f"], nf + 1)
                    link(d.tensor_tensor(c_, G[:, 1, 0:n_], c_, ALU.mult))
                    d.tensor_tensor(c_, c_, ig[s][:, 0:n_], ALU.add).then_inc(L_dve[s]["c"], 1)

            def hidden(k, u, s):
                p, st, half = UNITS[u]
                done = NU * k + u
                d.wait_ge(L_act[s]["o"], done + 1)
                d.wait_ge(L_act[s]["tc"], done + 1)
                dst = windows(2 * k + s, p, st, half) if st == p - 1 else shaped(ht[s], p)
                d.tensor_tensor(dst, shaped(Gt[s][:, 3, :], p), shaped(tc[s], p), ALU.mult)\
                 .then_inc(L_dve[s]["h"], 1)

            def item_sum(k, u, s):
                d.wait_ge(e_["t"], item(k, u, s) + 1)
                wait(d, st_out[u], 32 * (k - 1))
                x = X[:].rearrange("p (q b) j d -> p q (b j d)", b=2)[:, two_batches(k, u, s), :]
                d.tensor_tensor(u7[u][s][:].rearrange("p j d -> p (j d)"), bank[4 * s + 1][:], x, ALU.add)\
                 .then_inc(e_["u"], 1)

            def item_stats(k, u, s):
                d.wait_ge(e_["u"], item(k, u, s) + 1)
                for j in range(2 * J):
                    chain(d.bn_stats(bnE[u][s][:, j, :], u7[u][s][:, j, :]))
                chain.sync()
                for j in range(2 * J):
                    e = d.bn_aggr(mvE[u][s][:, j, :], bnE[u][s][:, j, :])
                    chain(e) if j < 2 * J - 1 else e.then_inc(e_["st"], 1)

            def item_norm(k, u, s):
                d.wait_ge(e_["rs"], item(k, u, s) + 1)
                for j in range(2 * J):
                    e = d.tensor_scalar(u7[u][s][:, j, :], u7[u][s][:, j, :], mvE[u][s][:, j, 0:1],
                                        rsE[u][s][:, j:j + 1], ALU.subtract, ALU.mult)
                    chain(e) if j < 2 * J - 1 else e.then_inc(e_["y"], 1)

            parts = {0: (item_sum, 0), 1: (item_sum, 1), 4: (item_stats, 0), 5: (item_stats, 1),
                     7: (item_norm, 0), 8: (item_norm, 1)}

            def pair(k, items=True):
                for u in range(NU):
                    for s in range(2):
                        cell(k, u, s)
                        hidden(k, u, s)
                        if items and u in parts:
                            part_of_item, iu = parts[u]
                            part_of_item(k, iu, s)
                chain.clear()
            pair(0, False)
            pair(1)
            with d.Fori(2, NG // 2) as k:
                pair(k)
            last = NG // 2
            for n_, (u, s) in enumerate(ITEMS):
                item_sum(last, u, s)
                item_stats(last, u, s)
                if n_:
                    item_norm(last, *ITEMS[n_ - 1])
            item_norm(last, *ITEMS[-1])


def kernel(**inputs):
    import numpy as np
    import concourse.bacc as bacc
    from concourse.bass_utils import run_bass_kernel_spmd

    lay = np.ascontiguousarray
    host = {n: lay(inputs[n]) for n in ROWS + SQUARES + ["x", "adj", "L0_gnn_W1", "L0_gnn_W2"] if n in inputs}
    host["L2_gnn_WvT"] = lay(inputs["L2_gnn_Wv"].T)
    for n, k in COLS.items():
        host[n] = lay(inputs[n].reshape(k, P).T)
    host["adjT"] = lay(inputs["adj"].T)
    host["L1_gnn_W1T"] = lay(inputs["L1_gnn_W1"].T)
    host["L1_gnn_W2T"] = lay(inputs["L1_gnn_W2"].T)
    host["L3_gnn_WihT"] = lay(inputs["L3_gnn_Wih"].transpose(0, 2, 1))
    host["L3_gnn_WhhT"] = lay(inputs["L3_gnn_Whh"].transpose(0, 2, 1))
    for n in ["L2_gnn_alpha", "L2_gnn_gamma"]:
        host[n] = lay(inputs[n]).reshape(1)
    nc = bacc.Bacc("TRN2", target_bir_lowering=False, num_devices=1)
    t = {n: nc.dram_tensor("in_" + n, a.shape, mybir.dt.from_np(a.dtype), kind="ExternalInput").ap()
         for n, a in host.items()}
    out = nc.dram_tensor("out_x", (B, N, D), F32, kind="ExternalOutput").ap()
    build(nc, t, out)
    r = run_bass_kernel_spmd(nc, [{"in_" + n: a for n, a in host.items()}], core_ids=[0])
    return r.results[0]["out_x"]
```
